# Optimizing a Trainium2 kernel written in Bass

```python
import numpy as np
import jax
import jax.numpy as jnp

def _softmax(x, axis=-1):
    return jax.nn.softmax(x, axis=axis)

def _gelu(x):
    return jax.nn.gelu(x, approximate=True)

def _silu(x):
    return jax.nn.silu(x)

def _sigmoid(x):
    return jax.nn.sigmoid(x)

def _layernorm(x, axis=-1, eps=1e-05):
    m = jnp.mean(x, axis=axis, keepdims=True)
    v = jnp.var(x, axis=axis, keepdims=True)
    return (x - m) / jnp.sqrt(v + eps)

def _scatter_add(tgt, idx, src, axis=0):
    return tgt.at[idx].add(src)

def _segment_sum(src, seg, n):
    return jax.ops.segment_sum(src, seg, n)
kernel_name = 'mk_dlrm_tower_d1_rec_r8_2b36f3'

def setup_inputs(seed: int=0):
    np.random.seed(seed)
    _w = jnp.asarray

    def _rec_inputs():
        import jax
        import jax.numpy as jnp
        _tk = jax.random.key(seed)
        dense_ctx = jax.random.normal(jax.random.fold_in(_tk, 190), (2048, 16), jnp.float32)
        ids = jnp.stack([jax.random.randint(jax.random.fold_in(_tk, 200 + f), (2048,), 0, v, jnp.int32) for f, v in enumerate([1250, 12500, 1000, 12500, 1250, 1250, 12500, 12500, 1000, 12500, 1250, 12500, 1250, 12500, 1000, 1000])], axis=1)
        tbl_0 = 0.05 * jax.random.normal(jax.random.fold_in(_tk, 500 + 0), (1250, 256), jnp.float32)
        tbl_1 = 0.05 * jax.random.normal(jax.random.fold_in(_tk, 500 + 1), (12500, 256), jnp.float32)
        tbl_2 = 0.05 * jax.random.normal(jax.random.fold_in(_tk, 500 + 2), (1000, 256), jnp.float32)
        tbl_3 = 0.05 * jax.random.normal(jax.random.fold_in(_tk, 500 + 3), (12500, 256), jnp.float32)
        tbl_4 = 0.05 * jax.random.normal(jax.random.fold_in(_tk, 500 + 4), (1250, 256), jnp.float32)
        tbl_5 = 0.05 * jax.random.normal(jax.random.fold_in(_tk, 500 + 5), (1250, 256), jnp.float32)
        tbl_6 = 0.05 * jax.random.normal(jax.random.fold_in(_tk, 500 + 6), (12500, 256), jnp.float32)
        tbl_7 = 0.05 * jax.random.normal(jax.random.fold_in(_tk, 500 + 7), (12500, 256), jnp.float32)
        tbl_8 = 0.05 * jax.random.normal(jax.random.fold_in(_tk, 500 + 8), (1000, 256), jnp.float32)
        tbl_9 = 0.05 * jax.random.normal(jax.random.fold_in(_tk, 500 + 9), (12500, 256), jnp.float32)
        tbl_10 = 0.05 * jax.random.normal(jax.random.fold_in(_tk, 500 + 10), (1250, 256), jnp.float32)
        tbl_11 = 0.05 * jax.random.normal(jax.random.fold_in(_tk, 500 + 11), (12500, 256), jnp.float32)
        tbl_12 = 0.05 * jax.random.normal(jax.random.fold_in(_tk, 500 + 12), (1250, 256), jnp.float32)
        tbl_13 = 0.05 * jax.random.normal(jax.random.fold_in(_tk, 500 + 13), (12500, 256), jnp.float32)
        tbl_14 = 0.05 * jax.random.normal(jax.random.fold_in(_tk, 500 + 14), (1000, 256), jnp.float32)
        tbl_15 = 0.05 * jax.random.normal(jax.random.fold_in(_tk, 500 + 15), (1000, 256), jnp.float32)
        _rk = jax.random.fold_in(_tk, 7)
        W_top1 = 0.125 * jax.random.normal(jax.random.fold_in(_tk, 801), (64, 512), jnp.float32)
        W_top2 = 0.0441942 * jax.random.normal(jax.random.fold_in(_tk, 802), (512, 256), jnp.float32)
        W_top3 = 0.0625 * jax.random.normal(jax.random.fold_in(_tk, 803), (256, 1), jnp.float32)
        b_top1 = jnp.zeros((512,), jnp.float32)
        b_top2 = jnp.zeros((256,), jnp.float32)
        return (dense_ctx, ids, tbl_0, tbl_1, tbl_2, tbl_3, tbl_4, tbl_5, tbl_6, tbl_7, tbl_8, tbl_9, tbl_10, tbl_11, tbl_12, tbl_13, tbl_14, tbl_15, W_top1, b_top1, W_top2, b_top2, W_top3)
    dense_ctx, ids, tbl_0, tbl_1, tbl_2, tbl_3, tbl_4, tbl_5, tbl_6, tbl_7, tbl_8, tbl_9, tbl_10, tbl_11, tbl_12, tbl_13, tbl_14, tbl_15, W_top1, b_top1, W_top2, b_top2, W_top3 = _rec_inputs()

    def _L0_rec_setup():
        import jax, jax.numpy as jnp
        import numpy as np
        B, F, E = (512, 16, 256)
        N_LAYERS = 3
        key = jax.random.key(seed)
        k1, k2, k3 = jax.random.split(key, 3)
        x = jax.random.normal(k1, (B, F, E), dtype=jnp.float32)
        Ws = jax.random.normal(k2, (N_LAYERS, F, F * F), dtype=jnp.float32) * 0.05
        bs = jax.random.normal(k3, (N_LAYERS, F), dtype=jnp.float32) * 0.05
        return {'x': x, 'Ws': Ws, 'bs': bs}
    _L0_rec_all = _L0_rec_setup()
    _L0_rec_in = {k: v for k, v in _L0_rec_all.items() if k in ('Ws', 'bs')}
    del _L0_rec_all
    return {'dense_ctx': dense_ctx, 'ids': ids, 'tbl_0': tbl_0, 'tbl_1': tbl_1, 'tbl_2': tbl_2, 'tbl_3': tbl_3, 'tbl_4': tbl_4, 'tbl_5': tbl_5, 'tbl_6': tbl_6, 'tbl_7': tbl_7, 'tbl_8': tbl_8, 'tbl_9': tbl_9, 'tbl_10': tbl_10, 'tbl_11': tbl_11, 'tbl_12': tbl_12, 'tbl_13': tbl_13, 'tbl_14': tbl_14, 'tbl_15': tbl_15, 'W_top1': W_top1, 'b_top1': b_top1, 'W_top2': W_top2, 'b_top2': b_top2, 'W_top3': W_top3, 'L0_rec_Ws': _L0_rec_in['Ws'], 'L0_rec_bs': _L0_rec_in['bs']}

def reference(dense_ctx, ids, tbl_0, tbl_1, tbl_2, tbl_3, tbl_4, tbl_5, tbl_6, tbl_7, tbl_8, tbl_9, tbl_10, tbl_11, tbl_12, tbl_13, tbl_14, tbl_15, W_top1, b_top1, W_top2, b_top2, W_top3, L0_rec_Ws, L0_rec_bs):
    import jax
    import jax.numpy as jnp

    def _L0_rec_ref(x, Ws, bs):
        import jax, jax.numpy as jnp
        import numpy as np
        B, F, E = (512, 16, 256)
        N_LAYERS = 3
        B_, F_, E_ = x.shape
        n_layers = Ws.shape[0]
        xk = x
        outs = []
        for i in range(n_layers):
            z = jnp.einsum('bfe,bge->bfge', x, xk).reshape(B_, F_ * F_, E_)
            z = jnp.swapaxes(z, 1, 2)
            z = jnp.einsum('bcl,oc->bol', z, Ws[i]) + bs[i][None, :, None]
            z = jax.nn.relu(z)
            z = jnp.sum(z, axis=-1)
            outs.append(z)
            xk = jnp.broadcast_to(z[:, :, None], (B_, F_, E_))
        return jnp.concatenate(outs, axis=1)
    e = jnp.stack([tbl_0[ids[:, 0]], tbl_1[ids[:, 1]], tbl_2[ids[:, 2]], tbl_3[ids[:, 3]], tbl_4[ids[:, 4]], tbl_5[ids[:, 5]], tbl_6[ids[:, 6]], tbl_7[ids[:, 7]], tbl_8[ids[:, 8]], tbl_9[ids[:, 9]], tbl_10[ids[:, 10]], tbl_11[ids[:, 11]], tbl_12[ids[:, 12]], tbl_13[ids[:, 13]], tbl_14[ids[:, 14]], tbl_15[ids[:, 15]]], axis=1)
    z = _L0_rec_ref(e, L0_rec_Ws, L0_rec_bs)
    z = z.reshape(z.shape[0], -1)
    h = jnp.concatenate([z, dense_ctx], axis=1)
    h = jnp.maximum(h @ W_top1 + b_top1, 0.0)
    h = jnp.maximum(h @ W_top2 + b_top2, 0.0)
    y = h @ W_top3
    return y

_drawn_inputs = setup_inputs


def setup_inputs(seed=0):
    import zlib

    import numpy as np

    out = dict(_drawn_inputs(seed))
    spreads = {'b_top1': (0.0, 2.0), 'b_top2': (0.0, 2.0)}
    factors = {'dense_ctx': 8.0}
    for name, (base, spread) in spreads.items():
        noise = np.random.default_rng([zlib.crc32(name.encode()), seed]).standard_normal(out[name].shape)
        drawn = base * np.exp(spread * noise) if base else spread * noise
        out[name] = jnp.asarray(drawn.astype(out[name].dtype))
    for name, factor in factors.items():
        out[name] = (out[name] * factor).astype(out[name].dtype)
    return out
```

```python
from contextlib import ExitStack

import numpy as np

import concourse.bass as bass
from concourse import mybir

FP32 = mybir.dt.float32
INT32 = mybir.dt.int32
UINT32 = mybir.dt.uint32
ALU = mybir.AluOpType
ACT = mybir.ActivationFunctionType
AX = mybir.AxisListType

VOCABS = [1250, 12500, 1000, 12500, 1250, 1250, 12500, 12500, 1000, 12500, 1250, 12500, 1250, 12500, 1000, 1000]

P = 128
BATCH = 2048
F = 16
E = 256
LAYERS = 3
EC = E // P
ROWS = P // F
TILES = BATCH // ROWS
QUAD = 4
QUADS = TILES // QUAD
GROUP = 16
SLOTS = GROUP // QUAD
GROUPS = TILES // GROUP
BLOCKS = QUAD * EC * ROWS
WRAP = F + F // 2
SHIFTS = F // 2
PAIRS = SHIFTS * F + F // 2
PAIR_TILES = 2
HALVES = QUAD // PAIR_TILES
LAG1 = SLOTS + 2
LAG2 = 3 * SLOTS + 1
DENSE = 16
HID1, HID2 = 512, 256
CHUNK = 512
CHUNKS = BATCH // CHUNK
CHUNK_TILES = TILES // CHUNKS
H1 = HID1 // P
H2 = HID2 // P
POOL_TILES = ((3,), (2, 3), (3,), (2, 3))


def at_least(eng, sem, value):
    if not isinstance(value, int) or value > 0:
        eng.wait_ge(sem, value)


def exists(n, count):
    return not isinstance(n, int) or 0 <= n < count


def build(nc, tables, ids_t, id_top, id_base, w_cols, biases, ident, block_ones, own_field,
          unpack_sel, dense_t, w_top1, b_top1, w_top2, b_top2, w_top3, y_out):
    ctx = ExitStack()
    with ctx:
        def sb(name, shape, dt=FP32):
            return ctx.enter_context(nc.sbuf_tensor(name, shape, dt))

        def ps(name, shape):
            return ctx.enter_context(nc.psum_tensor(name, shape, FP32))

        def sem(name):
            return ctx.enter_context(nc.semaphore(name))

        emb = sb("emb", [P, SLOTS, QUAD * E])
        emb_t = sb("emb_t", [P, 2, BLOCKS * WRAP])
        prods = sb("prods", [P, 2, QUAD, EC * ROWS * PAIRS])
        relu0 = sb("relu0", [P, 2, QUAD, PAIRS])
        sums0 = sb("sums0", [P, 2, 2, QUAD])
        proj = sb("proj", [P, TILES, 2, F])
        outer = sb("outer", [P, 2, 2, QUAD, F * F])
        z_all = sb("z_all", [P, LAYERS, TILES])
        z_diag = sb("z_diag", [P, 2, GROUP * F])
        z_rep = sb("z_rep", [P, 2, GROUP * F])
        ids_sb = sb("ids_sb", [P, TILES], INT32)
        rows_sb = sb("rows_sb", [P, TILES], INT32)
        rows_now = sb("rows_now", [P, GROUP], UINT32)
        id_lim = sb("id_lim", [P, 2], INT32)
        id_lim_f = sb("id_lim_f", [P, 2])
        w_sb = sb("w_sb", [P, LAYERS, EC, 2, 2 * F])
        bias_sb = sb("bias_sb", [P, LAYERS])
        ident_sb = sb("ident_sb", [P, P])
        ones_sb = sb("ones_sb", [P, P])
        own_sb = sb("own_sb", [P, F])
        unpack_sb = sb("unpack_sb", [P, LAYERS, ROWS, LAYERS * F])
        h0 = sb("h0", [LAYERS * F + DENSE, BATCH])
        w1_sb = sb("w1_sb", [LAYERS * F + DENSE, HID1])
        b1_sb = sb("b1_sb", [P, H1])
        w2_sb = sb("w2_sb", [P, H1, HID2])
        b2_sb = sb("b2_sb", [P, H2])
        w3_sb = sb("w3_sb", [P, H2])
        y_sb = sb("y_sb", [1, BATCH])
        h1 = sb("h1", [P, H1, CHUNK])
        h2 = sb("h2", [P, H2, CHUNK])

        turn_ps = ps("turn_ps", [P, 2, QUAD * E])
        sum_ps = ps("sum_ps", [P, HALVES, 512])
        proj_ps = ps("proj_ps", [P, 512])
        rep_ps = ps("rep_ps", [P, 512])

        ids_in = sem("ids_in")
        consts_in = sem("consts_in")
        top_in = sem("top_in")
        dve_setup = sem("dve_setup")
        rows_ready = sem("rows_ready")
        rows_copied = sem("rows_copied")
        gathered = [sem(f"gathered{j}") for j in range(SLOTS)]
        turned = sem("turned")
        emb_t_ready = sem("emb_t_ready")
        prods_dve = sem("prods_dve")
        prods_pool = sem("prods_pool")
        sums_done = sem("sums_done")
        relu0_ready = sem("relu0_ready")
        sums0_ready = sem("sums0_ready")
        proj_done = sem("proj_done")
        proj_ready = sem("proj_ready")
        z0_ready = sem("z0_ready")
        z_ready = [None, sem("z_ready1"), sem("z_ready2")]
        diag_ready = [sem(f"diag_ready{k}") for k in range(2)]
        rep_done = [sem(f"rep_done{k}") for k in range(2)]
        rep_ready = [sem(f"rep_ready{k}") for k in range(2)]
        outer_ready = [sem(f"outer_ready{k}") for k in range(2)]
        unpacked = sem("unpacked")
        h0_ready = sem("h0_ready")
        h1_done = sem("h1_done")
        h1_ready = sem("h1_ready")
        h2_done = sem("h2_done")
        h2_ready = sem("h2_ready")
        y_done = sem("y_done")
        y_ready = sem("y_ready")
        y_stored = sem("y_stored")

        N_CONSTS = 6
        N_TOP = 6
        LAST = GROUPS + 4
        PER = 2

        pool_tiles = [len(t) for t in POOL_TILES]
        pool_group = sum(pool_tiles) * PER
        dve_group = (GROUP - sum(pool_tiles)) * PER

        def pool_prods(g, j):
            return g * pool_group + sum(pool_tiles[:j + 1]) * PER

        def dve_prods(g, j):
            return g * dve_group + sum(QUAD - n for n in pool_tiles[:j + 1]) * PER

        def before(g, j, by):
            return g + (j - by) // SLOTS, (j - by) % SLOTS

        def multiply(eng, j, i, done):
            n = EC * ROWS
            x = emb_t[:, j % 2, i * n * WRAP:(i + 1) * n * WRAP].rearrange("p (n w) -> p n w", w=WRAP)
            out = prods[:, j % 2, i, :].rearrange("p (n k) -> p n k", k=PAIRS)
            step = [list(d) for d in x.ap]
            shifted = bass.AP(x.tensor, x.offset, [step[0], step[1], [1, SHIFTS], [1, F]])
            same = x[:, :, 0:F].rearrange("p n (u f) -> p n u f", u=1).broadcast_to([P, n, SHIFTS, F])
            eng.tensor_tensor(out[:, :, 0:SHIFTS * F].rearrange("p n (s f) -> p n s f", f=F), same, shifted,
                              ALU.mult).then_inc(done, 1)
            eng.tensor_tensor(out[:, :, SHIFTS * F:], x[:, :, 0:F // 2], x[:, :, F // 2:F], ALU.mult).then_inc(done, 1)

        def quad_products(eng, g, j, tiles, done):
            if exists(g, GROUPS):
                eng.wait_ge(emb_t_ready, 2 * (g * SLOTS + j + 1))
                at_least(eng, sums_done, HALVES * (g * SLOTS + j - 1))
                for i in tiles:
                    multiply(eng, j, i, done)

        def outer_products(eng, k, g, j):
            if exists(g, GROUPS):
                q = g * SLOTS + j
                eng.wait_ge(rep_ready[k], g + 1)
                at_least(eng, z_ready[k + 1], QUAD * (q - 1))
                y = proj[:, bass.ds(q * QUAD, QUAD), k, :]
                y = y.rearrange("p t (f u) -> p t f u", u=1).broadcast_to([P, QUAD, F, F])
                z = z_rep[:, k, j * QUAD * F:(j + 1) * QUAD * F].rearrange("p (t u f) -> p t u f", u=1, f=F)
                z = z.broadcast_to([P, QUAD, F, F])
                out = outer[:, k, j % 2, :, :].rearrange("p t (f g) -> p t f g", g=F)
                eng.tensor_tensor(out, y, z, ALU.mult).then_inc(outer_ready[k], 1)

        def spread(eng, k, g):
            if exists(g, GROUPS):
                if k == 0:
                    eng.wait_ge(z0_ready, (g + 1) * SLOTS)
                else:
                    eng.wait_ge(z_ready[1], (g + 1) * GROUP)
                at_least(eng, rep_ready[k], g)
                z = z_all[:, k, bass.ds(g * GROUP, GROUP)].rearrange("p (t u) -> p t u", u=1).broadcast_to([P, GROUP, F])
                m = own_sb[:].rearrange("p (u f) -> p u f", u=1).broadcast_to([P, GROUP, F])
                eng.tensor_tensor(z_diag[:, k, :].rearrange("p (t f) -> p t f", f=F), z, m, ALU.mult).then_inc(diag_ready[k], 1)

        block = ctx.enter_context(nc.Block())

        @block.sync
        def _(sp):
            sp.dma_start(ids_sb[:], ids_t).then_inc(ids_in, 16)
            sp.dma_start(id_lim[:, 0:1], id_top).then_inc(ids_in, 16)
            sp.dma_start(id_lim[:, 1:2], id_base).then_inc(ids_in, 16)
            sp.dma_start(ident_sb[:], ident).then_inc(consts_in, 16)
            sp.dma_start(w_sb[:], w_cols).then_inc(consts_in, 16)
            sp.dma_start(bias_sb[:], biases).then_inc(consts_in, 16)
            sp.dma_start(ones_sb[:], block_ones).then_inc(consts_in, 16)
            sp.dma_start(own_sb[:], own_field).then_inc(consts_in, 16)
            sp.dma_start(unpack_sb[:], unpack_sel).then_inc(consts_in, 16)
            sp.dma_start(h0[LAYERS * F:, :], dense_t).then_inc(top_in, 16)
            sp.dma_start(w1_sb[:], w_top1).then_inc(top_in, 16)
            sp.dma_start(b1_sb[:], b_top1).then_inc(top_in, 16)
            sp.dma_start(w2_sb[:], w_top2).then_inc(top_in, 16)
            sp.dma_start(b2_sb[:], b_top2).then_inc(top_in, 16)
            sp.dma_start(w3_sb[:], w_top3).then_inc(top_in, 16)
            sp.wait_ge(y_ready, CHUNKS)
            sp.dma_start(y_out, y_sb[:]).then_inc(y_stored, 16)
            sp.wait_ge(y_stored, 16)

        @block.gpsimd
        def _(pool):
            pool.wait_ge(rows_ready, 1)

            def take_rows(g, j):
                if exists(g, GROUPS):
                    q = g * SLOTS + j
                    at_least(pool, turned, q - SLOTS + 1)
                    at_least(pool, gathered[j], g * QUAD * 16)
                    nc.gpsimd.tensor_copy(rows_now[:, j * QUAD:(j + 1) * QUAD],
                                          rows_sb[:, bass.ds(q * QUAD, QUAD)].bitcast(UINT32)).then_inc(rows_copied, 1)

            def rows_taken(g, j):
                if exists(g, GROUPS):
                    pool.wait_ge(rows_copied, g * SLOTS + j + 1)

            def gather(g, j):
                if exists(g, GROUPS):
                    for i in range(QUAD):
                        nc.gpsimd.indirect_dma_start(
                            out=emb[:, j, i * E:(i + 1) * E], out_offset=None, in_=tables,
                            in_offset=bass.IndirectOffsetOnAxis(ap=rows_now[:, j * QUAD + i:j * QUAD + i + 1], axis=0),
                        ).then_inc(gathered[j], 16)

            def step(g):
                for j in range(SLOTS):
                    g3, j3 = before(g, j, -3)
                    take_rows(g3, j3)
                    rows_taken(g3, j3)
                    g1, j1 = before(g, j, -1)
                    quad_products(nc.gpsimd, g1, j1, POOL_TILES[j1], prods_pool)
                    gather(g3, j3)
                    outer_products(nc.gpsimd, 0, *before(g, j, LAG1))
                    outer_products(nc.gpsimd, 1, *before(g, j, LAG2))

            for j in range(3):
                take_rows(0, j)
            rows_taken(0, 2)
            for j in range(3):
                gather(0, j)
            pool.wait_ge(consts_in, N_CONSTS * 16)
            quad_products(nc.gpsimd, 0, 0, POOL_TILES[0], prods_pool)
            for g in range(4):
                step(g)
            with pool.Fori(4, GROUPS - 1) as g:
                step(g)
            for g in range(GROUPS - 1, LAST):
                step(g)

        @block.vector
        def _(dve):
            dve.wait_ge(ids_in, 3 * 16)
            nc.vector.tensor_copy(id_lim_f[:], id_lim[:]).then_inc(dve_setup, 1)
            dve.wait_ge(dve_setup, 1)
            nc.vector.tensor_scalar(rows_sb[:], ids_sb[:], 0.0, id_lim_f[:, 0:1], ALU.max, ALU.min).then_inc(dve_setup, 1)
            dve.wait_ge(dve_setup, 2)
            nc.vector.tensor_scalar(rows_sb[:], rows_sb[:], id_lim_f[:, 1:2], None, ALU.add).then_inc(rows_ready, 1)
            dve.wait_ge(consts_in, N_CONSTS * 16)

            def reduce0(g, j):
                if exists(g, GROUPS):
                    q = g * SLOTS + j
                    dve.wait_ge(relu0_ready, HALVES * (q + 1))
                    at_least(dve, z0_ready, q - 1)
                    nc.vector.tensor_reduce(sums0[:, j % 2, 0, :], relu0[:, j % 2, :, F:], AX.X, ALU.add).then_inc(sums0_ready, 1)
                    nc.vector.tensor_reduce(sums0[:, j % 2, 1, :], relu0[:, j % 2, :, 0:F], AX.X, ALU.add).then_inc(sums0_ready, 1)
                    dve.wait_ge(sums0_ready, 2 * (q + 1))
                    nc.vector.scalar_tensor_tensor(out=z_all[:, 0, bass.ds(q * QUAD, QUAD)], in0=sums0[:, j % 2, 0, :],
                                                   scalar=2.0, in1=sums0[:, j % 2, 1, :],
                                                   op0=ALU.mult, op1=ALU.add).then_inc(z0_ready, 1)

            def step(g):
                for j in range(SLOTS):
                    g1, j1 = before(g, j, -1)
                    reduce0(*before(g, j, 1))
                    if j == 0:
                        spread(nc.vector, 0, g - 1)
                    if j == 3:
                        spread(nc.vector, 1, g - 2)
                    quad_products(nc.vector, g1, j1, [i for i in range(QUAD) if i not in POOL_TILES[j1]], prods_dve)

            quad_products(nc.vector, 0, 0, [i for i in range(QUAD) if i not in POOL_TILES[0]], prods_dve)
            for g in range(4):
                step(g)
            with dve.Fori(4, GROUPS - 1) as g:
                step(g)
            for g in range(GROUPS - 1, LAST):
                step(g)

        @block.scalar
        def _(act):
            act.wait_ge(consts_in, N_CONSTS * 16)

            def take_turned(g, j):
                if exists(g, GROUPS):
                    q = g * SLOTS + j
                    act.wait_ge(turned, q + 1)
                    if exists(g * SLOTS + j - 2, QUADS):
                        g2, j2 = before(g, j, 2)
                        act.wait_ge(prods_dve, dve_prods(g2, j2))
                        act.wait_ge(prods_pool, pool_prods(g2, j2))
                        act.wait_ge(proj_done, q - 1)
                    src = turn_ps[:, j % 2, :].rearrange("p (n f) -> p n f", f=F)
                    out = emb_t[:, j % 2, :].rearrange("p (n w) -> p n w", w=WRAP)
                    nc.scalar.copy(out[:, :, 0:F], src).then_inc(emb_t_ready, 1)
                    nc.scalar.copy(out[:, :, F:WRAP], src[:, :, 0:F // 2]).then_inc(emb_t_ready, 1)

            def take_proj(g, j):
                if exists(g, GROUPS):
                    q = g * SLOTS + j
                    act.wait_ge(proj_done, q + 1)
                    nc.scalar.copy(proj[:, bass.ds(q * QUAD, QUAD), :, :],
                                   proj_ps[:, 0:QUAD * 2 * F].rearrange("p (k t f) -> p t k f", k=2, f=F)).then_inc(proj_ready, 1)

            def relu_pairs(g, j):
                if exists(g, GROUPS):
                    q = g * SLOTS + j
                    for h in range(HALVES):
                        act.wait_ge(sums_done, HALVES * q + h + 1)
                        at_least(act, z0_ready, q - 1)
                        nc.scalar.activation(relu0[:, j % 2, h * PAIR_TILES:(h + 1) * PAIR_TILES, :],
                                             sum_ps[:, h, 0:PAIR_TILES * PAIRS].rearrange("p (t k) -> p t k", k=PAIRS),
                                             ACT.Relu, bias=bias_sb[:, 0:1]).then_inc(relu0_ready, 1)

            def relu_outer(k, g, j):
                if exists(g, GROUPS):
                    q = g * SLOTS + j
                    act.wait_ge(outer_ready[k], q + 1)
                    for i in range(QUAD):
                        x = outer[:, k, j % 2, i, :]
                        nc.scalar.activation(x, x, ACT.Relu, bias=bias_sb[:, k + 1:k + 2],
                                             accum_out=z_all[:, k + 1, bass.ds(q * QUAD + i, 1)]).then_inc(z_ready[k + 1], 1)

            def take_rep(k, g):
                if exists(g, GROUPS):
                    act.wait_ge(rep_done[k], g + 1)
                    at_least(act, outer_ready[k], g * SLOTS)
                    nc.scalar.copy(z_rep[:, k, :], rep_ps[:, 0:GROUP * F]).then_inc(rep_ready[k], 1)

            def step(g):
                for j in range(SLOTS):
                    take_turned(*before(g, j, -2))
                    if j == 1:
                        take_rep(0, g - 1)
                    if j == 0:
                        take_rep(1, g - 3)
                    relu_pairs(*before(g, j, 1))
                    relu_outer(0, *before(g, j, LAG1 + 1))
                    relu_outer(1, *before(g, j, LAG2 + 1))
                    take_proj(*before(g, j, -1))

            take_turned(0, 0)
            take_turned(0, 1)
            take_proj(0, 0)
            for g in range(4):
                step(g)
            with act.Fori(4, GROUPS - 1) as g:
                step(g)
            for g in range(GROUPS - 1, LAST):
                step(g)

            act.wait_ge(top_in, N_TOP * 16)
            for c in range(CHUNKS):
                act.wait_ge(unpacked, c + 1)
                nc.scalar.copy(h0[0:LAYERS * F, c * CHUNK:(c + 1) * CHUNK], rep_ps[0:LAYERS * F, :]).then_inc(h0_ready, 1)
                for i in range(H1):
                    act.wait_ge(h1_done, c * H1 + i + 1)
                    if c > 0:
                        act.wait_ge(h2_done, c * H2)
                    nc.scalar.activation(h1[:, i, :], turn_ps[:, i // 2, i % 2 * 512:(i % 2 + 1) * 512], ACT.Relu,
                                         bias=b1_sb[:, i:i + 1]).then_inc(h1_ready, 1)
                for i in range(H2):
                    act.wait_ge(h2_done, c * H2 + i + 1)
                    if c > 0:
                        act.wait_ge(y_done, c)
                    nc.scalar.activation(h2[:, i, :], sum_ps[:, i, :], ACT.Relu, bias=b2_sb[:, i:i + 1]).then_inc(h2_ready, 1)
                act.wait_ge(y_done, c + 1)
                nc.scalar.copy(y_sb[:, c * CHUNK:(c + 1) * CHUNK], proj_ps[0:1, :]).then_inc(y_ready, 1)

        @block.tensor
        def _(pe):
            pe.wait_ge(consts_in, N_CONSTS * 16)

            def turn(g, j):
                if exists(g, GROUPS):
                    q = g * SLOTS + j
                    pe.wait_ge(gathered[j], (g + 1) * QUAD * 16)
                    at_least(pe, emb_t_ready, 2 * (q - 1))
                    for i in range(QUAD * EC):
                        last = nc.tensor.transpose(turn_ps[:, j % 2, i * P:(i + 1) * P], emb[:, j, i * P:(i + 1) * P], ident_sb[:])
                    last.then_inc(turned, 1)

            def sum_pairs(g, j):
                if exists(g, GROUPS):
                    q = g * SLOTS + j
                    pe.wait_ge(prods_dve, dve_prods(g, j))
                    pe.wait_ge(prods_pool, pool_prods(g, j))
                    for h in range(HALVES):
                        at_least(pe, relu0_ready, HALVES * (q - 1) + h + 1)
                        x = prods[:, j % 2, h * PAIR_TILES:(h + 1) * PAIR_TILES, :]
                        x = x.rearrange("p t (c r k) -> p c r t k", c=EC, r=ROWS)
                        for c in range(EC):
                            for odd in range(2):
                                for s in range(ROWS // 2):
                                    last = nc.tensor.matmul(
                                        sum_ps[s * 2 * F:(s + 1) * 2 * F, h, 0:PAIR_TILES * PAIRS], w_sb[:, 0, c, odd, :],
                                        x[:, c, 2 * s + odd, :, :], start=c == 0 and odd == 0, stop=c == EC - 1 and odd == 1)
                        last.then_inc(sums_done, 1)

            def project(g, j):
                if exists(g, GROUPS):
                    q = g * SLOTS + j
                    pe.wait_ge(emb_t_ready, 2 * (q + 1))
                    at_least(pe, proj_ready, q)
                    x = emb_t[:, j % 2, :].rearrange("p (t c r w) -> p c r t w", t=QUAD, c=EC, r=ROWS)
                    for k in range(2):
                        for c in range(EC):
                            for odd in range(2):
                                for s in range(ROWS // 2):
                                    last = nc.tensor.matmul(
                                        proj_ps[s * 2 * F:(s + 1) * 2 * F, k * QUAD * F:(k + 1) * QUAD * F],
                                        w_sb[:, k + 1, c, odd, :], x[:, c, 2 * s + odd, :, 0:F],
                                        start=c == 0 and odd == 0, stop=c == EC - 1 and odd == 1)
                    last.then_inc(proj_done, 1)

            def repeat_z(k, g):
                if exists(g, GROUPS):
                    pe.wait_ge(diag_ready[k], g + 1)
                    if k == 0:
                        at_least(pe, rep_ready[1], g - 1)
                    else:
                        pe.wait_ge(rep_ready[0], min(g + 2, GROUPS) if isinstance(g, int) else g + 2)
                    nc.tensor.matmul(rep_ps[:, 0:GROUP * F], ones_sb[:], z_diag[:, k, :], start=True, stop=True).then_inc(rep_done[k], 1)

            def step(g):
                for j in range(SLOTS):
                    turn(*before(g, j, -2))
                    if j == 0:
                        repeat_z(1, g - 3)
                    if j == 1:
                        repeat_z(0, g - 1)
                    sum_pairs(g, j)
                    project(*before(g, j, -1))

            turn(0, 0)
            turn(0, 1)
            project(0, 0)
            for g in range(4):
                step(g)
            with pe.Fori(4, GROUPS - 1) as g:
                step(g)
            for g in range(GROUPS - 1, LAST):
                step(g)

            pe.wait_ge(top_in, N_TOP * 16)
            pe.wait_ge(z_ready[2], TILES)
            pe.wait_ge(rep_ready[1], GROUPS)
            for c in range(CHUNKS):
                if c > 0:
                    pe.wait_ge(h0_ready, c)
                for r in range(ROWS):
                    for k in range(LAYERS):
                        last = nc.tensor.matmul(rep_ps[0:LAYERS * F, r * CHUNK_TILES:(r + 1) * CHUNK_TILES], unpack_sb[:, k, r, :],
                                                z_all[:, k, c * CHUNK_TILES:(c + 1) * CHUNK_TILES], start=k == 0, stop=k == LAYERS - 1)
                last.then_inc(unpacked, 1)
                pe.wait_ge(h0_ready, c + 1)
                for i in range(H1):
                    if c > 0:
                        pe.wait_ge(h1_ready, (c - 1) * H1 + i + 1)
                    nc.tensor.matmul(turn_ps[:, i // 2, i % 2 * 512:(i % 2 + 1) * 512], w1_sb[:, i * P:(i + 1) * P],
                                     h0[:, c * CHUNK:(c + 1) * CHUNK], start=True, stop=True).then_inc(h1_done, 1)
                for i in range(H2):
                    if c > 0:
                        pe.wait_ge(h2_ready, (c - 1) * H2 + i + 1)
                    for a in range(H1):
                        pe.wait_ge(h1_ready, c * H1 + a + 1)
                        last = nc.tensor.matmul(sum_ps[:, i, :], w2_sb[:, a, i * P:(i + 1) * P], h1[:, a, :],
                                                start=a == 0, stop=a == H1 - 1)
                    last.then_inc(h2_done, 1)
                if c > 0:
                    pe.wait_ge(y_ready, c)
                for i in range(H2):
                    pe.wait_ge(h2_ready, c * H2 + i + 1)
                    last = nc.tensor.matmul(proj_ps[0:1, :], w3_sb[:, i:i + 1], h2[:, i, :], start=i == 0, stop=i == H2 - 1)
                last.then_inc(y_done, 1)


def shape_constants():
    row_of = np.arange(P) // F
    unpack = np.zeros((ROWS, F, LAYERS, ROWS, LAYERS, F), np.float32)
    for r in range(ROWS):
        for k in range(LAYERS):
            unpack[r, range(F), k, r, k, range(F)] = 1.0
    return dict(
        id_top=np.tile(np.array(VOCABS, np.int32) - 1, ROWS).reshape(P, 1),
        id_base=np.tile(np.cumsum([0] + VOCABS[:-1]).astype(np.int32), ROWS).reshape(P, 1),
        ident=np.eye(P, dtype=np.float32), block_ones=(row_of[:, None] == row_of[None, :]).astype(np.float32),
        own_field=np.tile(np.eye(F, dtype=np.float32), (ROWS, 1)),
        unpack_sel=unpack.reshape(P, LAYERS, ROWS, LAYERS * F))


def kernel(**inputs):
    import concourse.bacc as bacc
    from concourse.bass_utils import run_bass_kernel_spmd

    x = {name: np.asarray(a) for name, a in inputs.items()}
    ids = x["ids"].reshape(ROWS, TILES, F).transpose(0, 2, 1).reshape(P, TILES)
    w = x["L0_rec_Ws"].reshape(LAYERS, F, EC, P).transpose(3, 0, 2, 1)
    w_cols = np.zeros((P, LAYERS, EC, 2, 2 * F), w.dtype)
    w_cols[:, :, :, 0, :F] = w
    w_cols[:, :, :, 1, F:] = w
    dense = x["dense_ctx"].reshape(ROWS, CHUNKS, CHUNK_TILES, DENSE).transpose(3, 1, 0, 2).reshape(DENSE, BATCH)
    const = shape_constants()
    arrays = {
        "tables": np.concatenate([x[f"tbl_{i}"] for i in range(F)], axis=0),
        "ids_t": ids, "id_top": const["id_top"], "id_base": const["id_base"],
        "w_cols": w_cols, "biases": np.tile(x["L0_rec_bs"].T, (ROWS, 1)),
        "ident": const["ident"], "block_ones": const["block_ones"], "own_field": const["own_field"],
        "unpack_sel": const["unpack_sel"], "dense_t": dense,
        "w_top1": x["W_top1"], "b_top1": x["b_top1"].reshape(H1, P).T,
        "w_top2": x["W_top2"].reshape(H1, P, HID2).transpose(1, 0, 2), "b_top2": x["b_top2"].reshape(H2, P).T,
        "w_top3": x["W_top3"].reshape(H2, P).T,
    }
    arrays = {name: np.ascontiguousarray(a) for name, a in arrays.items()}
    nc = bacc.Bacc("TRN2", target_bir_lowering=False, num_devices=1)
    args = [nc.dram_tensor(name, a.shape, mybir.dt.from_np(a.dtype), kind="ExternalInput").ap() for name, a in arrays.items()]
    y = nc.dram_tensor("y", (1, BATCH), FP32, kind="ExternalOutput").ap()
    build(nc, *args, y)
    r = run_bass_kernel_spmd(nc, [arrays], core_ids=[0])
    got = r.results[0]["y"].reshape(CHUNKS, ROWS, CHUNK_TILES)
    return got.transpose(1, 0, 2).reshape(BATCH, 1)
```

```python
from contextlib import ExitStack

import numpy as np

import concourse.bass as bass
from concourse import mybir

FP32 = mybir.dt.float32
INT32 = mybir.dt.int32
UINT32 = mybir.dt.uint32
ALU = mybir.AluOpType
ACT = mybir.ActivationFunctionType
AX = mybir.AxisListType

VOCABS = [1250, 12500, 1000, 12500, 1250, 1250, 12500, 12500, 1000, 12500, 1250, 12500, 1250, 12500, 1000, 1000]

P = 128
BATCH = 2048
F = 16
E = 256
LAYERS = 3
EC = E // P
ROWS = P // F
TILES = BATCH // ROWS
QUAD = 4
QUADS = TILES // QUAD
GROUP = 16
SLOTS = GROUP // QUAD
GROUPS = TILES // GROUP
BLOCKS = QUAD * EC * ROWS
WRAP = F + F // 2
SHIFTS = F // 2
PAIRS = SHIFTS * F + F // 2
PAIR_TILES = 2
HALVES = QUAD // PAIR_TILES
LAG1 = SLOTS + 3
LAG2 = 3 * SLOTS + 1
DENSE = 16
HID1, HID2 = 512, 256
CHUNK = 512
CHUNKS = BATCH // CHUNK
CHUNK_TILES = TILES // CHUNKS
H1 = HID1 // P
H2 = HID2 // P
PER_TILE = EC * ROWS
DVE_BLOCKS = (BLOCKS, BLOCKS, BLOCKS, BLOCKS - PER_TILE // 2)
POOL_SLOTS = [j for j in range(SLOTS) if DVE_BLOCKS[j] < BLOCKS]
RELUS0 = QUAD + 1


def at_least(eng, sem, value):
    if not isinstance(value, int) or value > 0:
        eng.wait_ge(sem, value)


def exists(n, count):
    return not isinstance(n, int) or 0 <= n < count


def build(nc, tables, ids_t, id_top, id_base, w_cols, biases, ident, block_ones, own_field,
          unpack_sel, dense_t, w_top1, b_top1, w_top2, b_top2, w_top3, y_out):
    ctx = ExitStack()
    with ctx:
        def sb(name, shape, dt=FP32):
            return ctx.enter_context(nc.sbuf_tensor(name, shape, dt))

        def ps(name, shape):
            return ctx.enter_context(nc.psum_tensor(name, shape, FP32))

        def sem(name):
            return ctx.enter_context(nc.semaphore(name))

        emb = sb("emb", [P, SLOTS, QUAD * E])
        emb_t = sb("emb_t", [P, SLOTS, BLOCKS * WRAP])
        prods = sb("prods", [P, 2, QUAD, EC * ROWS * PAIRS])
        relu0 = sb("relu0", [P, QUAD, PAIRS - F])
        own0 = sb("own0", [P, GROUP, F])
        own_sum0 = sb("own_sum0", [P, GROUP])
        proj = sb("proj", [P, TILES, 2, F])
        outer = sb("outer", [P, 2, 2, QUAD, F * F])
        z_all = sb("z_all", [P, LAYERS, TILES])
        z_diag = sb("z_diag", [P, 2, GROUP * F])
        z_rep = sb("z_rep", [P, 2, GROUP * F])
        ids_sb = sb("ids_sb", [P, TILES], INT32)
        rows_sb = sb("rows_sb", [P, TILES], INT32)
        rows_now = sb("rows_now", [P, GROUP], UINT32)
        id_lim = sb("id_lim", [P, 2], INT32)
        id_lim_f = sb("id_lim_f", [P, 2])
        w_sb = sb("w_sb", [P, LAYERS, EC, 2, 2 * F])
        bias_sb = sb("bias_sb", [P, LAYERS])
        ident_sb = sb("ident_sb", [P, P])
        ones_sb = sb("ones_sb", [P, P])
        own_sb = sb("own_sb", [P, F])
        unpack_sb = sb("unpack_sb", [P, LAYERS, ROWS, LAYERS * F])
        h0 = sb("h0", [LAYERS * F + DENSE, BATCH])
        w1_sb = sb("w1_sb", [LAYERS * F + DENSE, HID1])
        b1_sb = sb("b1_sb", [P, H1])
        w2_sb = sb("w2_sb", [P, H1, HID2])
        b2_sb = sb("b2_sb", [P, H2])
        w3_sb = sb("w3_sb", [P, H2])
        y_sb = sb("y_sb", [1, 2, CHUNK])
        h1 = sb("h1", [P, H1, CHUNK])
        h2 = sb("h2", [P, H2, CHUNK])

        turn_ps = ps("turn_ps", [P, 2, QUAD * E])
        sum_ps = ps("sum_ps", [P, HALVES, 512])
        proj_ps = ps("proj_ps", [P, 512])
        rep_ps = ps("rep_ps", [P, 512])

        ids_in = sem("ids_in")
        consts_in = sem("consts_in")
        top_in = sem("top_in")
        dve_setup = sem("dve_setup")
        rows_ready = sem("rows_ready")
        rows_copied = sem("rows_copied")
        gathered = [sem(f"gathered{j}") for j in range(SLOTS)]
        turned = sem("turned")
        emb_t_ready = sem("emb_t_ready")
        prods_dve = sem("prods_dve")
        prods_pool = sem("prods_pool")
        sums_done = sem("sums_done")
        relu0_ready = sem("relu0_ready")
        own_sum_ready = sem("own_sum_ready")
        proj_done = sem("proj_done")
        proj_ready = sem("proj_ready")
        z0_ready = sem("z0_ready")
        z_ready = [None, sem("z_ready1"), sem("z_ready2")]
        diag_ready = [sem(f"diag_ready{k}") for k in range(2)]
        rep_done = [sem(f"rep_done{k}") for k in range(2)]
        rep_ready = [sem(f"rep_ready{k}") for k in range(2)]
        outer_ready = [sem(f"outer_ready{k}") for k in range(2)]
        unpacked = sem("unpacked")
        h0_ready = sem("h0_ready")
        h1_done = sem("h1_done")
        h1_ready = sem("h1_ready")
        h2_done = sem("h2_done")
        h2_ready = sem("h2_ready")
        y_done = sem("y_done")
        y_ready = sem("y_ready")
        y_stored = sem("y_stored")

        N_CONSTS = 6
        N_TOP = 6
        LAST = GROUPS + 4

        def made(g, j):
            return 2 * (g * SLOTS + j + 1)

        def made_pool(g, j):
            return 2 * (g * len(POOL_SLOTS) + len([s for s in POOL_SLOTS if s <= j]))

        def before(g, j, by):
            return g + (j - by) // SLOTS, (j - by) % SLOTS

        def multiply(eng, j, b0, b1, own, done):
            x = emb_t[:, j, :].rearrange("p (n w) -> p n w", w=WRAP)[:, b0:b1, :]
            out = prods[:, j % 2, :, :].rearrange("p t (n k) -> p (t n) k", k=PAIRS)[:, b0:b1, :]
            step = [list(d) for d in x.ap]
            shifted = bass.AP(x.tensor, x.offset, [step[0], step[1], [1, SHIFTS], [1, F]])
            same = own[:, b0:b1, :]
            every = same[:, :, 0:F].rearrange("p n (u f) -> p n u f", u=1).broadcast_to([P, b1 - b0, SHIFTS, F])
            eng.tensor_tensor(out[:, :, 0:SHIFTS * F].rearrange("p n (s f) -> p n s f", f=F), every, shifted,
                              ALU.mult).then_inc(done, 1)
            eng.tensor_tensor(out[:, :, SHIFTS * F:], same[:, :, 0:F // 2], x[:, :, F // 2:F], ALU.mult).then_inc(done, 1)

        def quad_waits(eng, g, j):
            eng.wait_ge(emb_t_ready, 2 * (g * SLOTS + j + 1))
            at_least(eng, sums_done, HALVES * (g * SLOTS + j - 1))

        def outer_products(eng, k, g, j):
            if exists(g, GROUPS):
                q = g * SLOTS + j
                eng.wait_ge(rep_ready[k], g + 1)
                at_least(eng, z_ready[k + 1], QUAD * (q - 1))
                y = proj[:, bass.ds(q * QUAD, QUAD), k, :]
                y = y.rearrange("p t (f u) -> p t f u", u=1).broadcast_to([P, QUAD, F, F])
                z = z_rep[:, k, j * QUAD * F:(j + 1) * QUAD * F].rearrange("p (t u f) -> p t u f", u=1, f=F)
                z = z.broadcast_to([P, QUAD, F, F])
                out = outer[:, k, j % 2, :, :].rearrange("p t (f g) -> p t f g", g=F)
                eng.tensor_tensor(out, y, z, ALU.mult).then_inc(outer_ready[k], 1)

        def spread(eng, k, g):
            if exists(g, GROUPS):
                if k == 0:
                    eng.wait_ge(z0_ready, g + 1)
                else:
                    eng.wait_ge(z_ready[1], (g + 1) * GROUP)
                at_least(eng, rep_ready[k], g)
                z = z_all[:, k, bass.ds(g * GROUP, GROUP)].rearrange("p (t u) -> p t u", u=1).broadcast_to([P, GROUP, F])
                m = own_sb[:].rearrange("p (u f) -> p u f", u=1).broadcast_to([P, GROUP, F])
                eng.tensor_tensor(z_diag[:, k, :].rearrange("p (t f) -> p t f", f=F), z, m, ALU.mult).then_inc(diag_ready[k], 1)

        block = ctx.enter_context(nc.Block())

        @block.sync
        def _(sp):
            sp.dma_start(ids_sb[:], ids_t).then_inc(ids_in, 16)
            sp.dma_start(id_lim[:, 0:1], id_top).then_inc(ids_in, 16)
            sp.dma_start(id_lim[:, 1:2], id_base).then_inc(ids_in, 16)
            sp.dma_start(ident_sb[:], ident).then_inc(consts_in, 16)
            sp.dma_start(w_sb[:], w_cols).then_inc(consts_in, 16)
            sp.dma_start(bias_sb[:], biases).then_inc(consts_in, 16)
            sp.dma_start(ones_sb[:], block_ones).then_inc(consts_in, 16)
            sp.dma_start(own_sb[:], own_field).then_inc(consts_in, 16)
            sp.dma_start(unpack_sb[:], unpack_sel).then_inc(consts_in, 16)
            sp.dma_start(h0[LAYERS * F:, :], dense_t).then_inc(top_in, 16)
            sp.dma_start(w1_sb[:], w_top1).then_inc(top_in, 16)
            sp.dma_start(b1_sb[:], b_top1).then_inc(top_in, 16)
            sp.dma_start(w2_sb[:], w_top2).then_inc(top_in, 16)
            sp.dma_start(b2_sb[:], b_top2).then_inc(top_in, 16)
            sp.dma_start(w3_sb[:], w_top3).then_inc(top_in, 16)
            for c in range(CHUNKS):
                sp.wait_ge(y_ready, c + 1)
                sp.dma_start(y_out[:, c * CHUNK:(c + 1) * CHUNK], y_sb[:, c % 2, :]).then_inc(y_stored, 16)
                sp.wait_ge(y_stored, 16 * (c + 1))

        @block.gpsimd
        def _(pool):
            pool.wait_ge(rows_ready, 1)

            def take_rows(g, j):
                if exists(g, GROUPS):
                    q = g * SLOTS + j
                    at_least(pool, turned, q - SLOTS + 1)
                    at_least(pool, gathered[j], g * QUAD * 16)
                    nc.gpsimd.tensor_copy(rows_now[:, j * QUAD:(j + 1) * QUAD],
                                          rows_sb[:, bass.ds(q * QUAD, QUAD)].bitcast(UINT32)).then_inc(rows_copied, 1)

            def rows_taken(g, j):
                if exists(g, GROUPS):
                    pool.wait_ge(rows_copied, g * SLOTS + j + 1)

            def gather(g, j):
                if exists(g, GROUPS):
                    for i in range(QUAD):
                        nc.gpsimd.indirect_dma_start(
                            out=emb[:, j, i * E:(i + 1) * E], out_offset=None, in_=tables,
                            in_offset=bass.IndirectOffsetOnAxis(ap=rows_now[:, j * QUAD + i:j * QUAD + i + 1], axis=0),
                        ).then_inc(gathered[j], 16)

            def products(g, j):
                if exists(g, GROUPS) and j in POOL_SLOTS:
                    quad_waits(pool, g, j)
                    multiply(nc.gpsimd, j, DVE_BLOCKS[j], BLOCKS, emb_t[:, j, :].rearrange("p (n w) -> p n w", w=WRAP), prods_pool)

            def step(g):
                for j in range(SLOTS):
                    g3, j3 = before(g, j, -3)
                    take_rows(g3, j3)
                    rows_taken(g3, j3)
                    g1, j1 = before(g, j, -1)
                    products(g1, j1)
                    outer_products(nc.gpsimd, 0, *before(g, j, LAG1))
                    gather(g3, j3)
                    outer_products(nc.gpsimd, 1, *before(g, j, LAG2))

            for j in range(3):
                take_rows(0, j)
            rows_taken(0, 2)
            for j in range(3):
                gather(0, j)
            pool.wait_ge(consts_in, N_CONSTS * 16)
            products(0, 0)
            for g in range(4):
                step(g)
            with pool.Fori(4, GROUPS - 1) as g:
                step(g)
            for g in range(GROUPS - 1, LAST):
                step(g)

        @block.vector
        def _(dve):
            dve.wait_ge(ids_in, 3 * 16)
            nc.vector.tensor_copy(id_lim_f[:], id_lim[:]).then_inc(dve_setup, 1)
            dve.wait_ge(dve_setup, 1)
            nc.vector.tensor_scalar(rows_sb[:], ids_sb[:], 0.0, id_lim_f[:, 0:1], ALU.max, ALU.min).then_inc(dve_setup, 1)
            dve.wait_ge(dve_setup, 2)
            nc.vector.tensor_scalar(rows_sb[:], rows_sb[:], id_lim_f[:, 1:2], None, ALU.add).then_inc(rows_ready, 1)
            dve.wait_ge(consts_in, N_CONSTS * 16)

            def finish0(g):
                if exists(g, GROUPS):
                    dve.wait_ge(relu0_ready, RELUS0 * SLOTS * (g + 1))
                    nc.vector.tensor_reduce(own_sum0[:], own0[:], AX.X, ALU.add).then_inc(own_sum_ready, 1)
                    dve.wait_ge(own_sum_ready, g + 1)
                    z = z_all[:, 0, bass.ds(g * GROUP, GROUP)]
                    nc.vector.scalar_tensor_tensor(out=z, in0=z, scalar=2.0, in1=own_sum0[:],
                                                   op0=ALU.mult, op1=ALU.add).then_inc(z0_ready, 1)

            def products(g, j):
                if exists(g, GROUPS):
                    quad_waits(dve, g, j)
                    multiply(nc.vector, j, 0, DVE_BLOCKS[j], turn_ps[:, j % 2, :].rearrange("p (n f) -> p n f", f=F), prods_dve)

            def step(g):
                for j in range(SLOTS):
                    products(*before(g, j, -1))
                    if j == 0:
                        spread(nc.vector, 1, g - 3)
                        finish0(g - 1)
                    if j == 1:
                        spread(nc.vector, 0, g - 1)

            products(0, 0)
            for g in range(4):
                step(g)
            with dve.Fori(4, GROUPS - 1) as g:
                step(g)
            for g in range(GROUPS - 1, LAST):
                step(g)

        @block.scalar
        def _(act):
            act.wait_ge(consts_in, N_CONSTS * 16)

            def take_turned(g, j):
                if exists(g, GROUPS):
                    q = g * SLOTS + j
                    act.wait_ge(turned, q + 1)
                    at_least(act, prods_dve, made(g - 1, j))
                    if j in POOL_SLOTS:
                        at_least(act, prods_pool, made_pool(g - 1, j))
                    at_least(act, proj_done, g)
                    src = turn_ps[:, j % 2, :].rearrange("p (n f) -> p n f", f=F)
                    out = emb_t[:, j, :].rearrange("p (n w) -> p n w", w=WRAP)
                    nc.scalar.copy(out[:, :, 0:F], src).then_inc(emb_t_ready, 1)
                    nc.scalar.copy(out[:, :, F:WRAP], src[:, :, 0:F // 2]).then_inc(emb_t_ready, 1)

            def take_proj(g):
                if exists(g, GROUPS):
                    act.wait_ge(proj_done, g + 1)
                    nc.scalar.copy(proj[:, bass.ds(g * GROUP, GROUP), :, :],
                                   proj_ps[:].rearrange("p (k t f) -> p t k f", k=2, f=F)).then_inc(proj_ready, 1)

            def relu_pairs(g, j):
                if exists(g, GROUPS):
                    q = g * SLOTS + j
                    for i in range(QUAD):
                        h, t = i // PAIR_TILES, i % PAIR_TILES
                        act.wait_ge(sums_done, HALVES * q + h + 1)
                        nc.scalar.activation(relu0[:, i, :], sum_ps[:, h, t * PAIRS + F:(t + 1) * PAIRS], ACT.Relu,
                                             bias=bias_sb[:, 0:1], accum_out=z_all[:, 0, bass.ds(q * QUAD + i, 1)]).then_inc(relu0_ready, 1)
                    at_least(act, own_sum_ready, g)
                    own = sum_ps[:, :, 0:PAIR_TILES * PAIRS].rearrange("p h (t k) -> p h t k", k=PAIRS)[:, :, :, 0:F]
                    nc.scalar.activation(own0[:, j * QUAD:(j + 1) * QUAD, :].rearrange("p (h t) f -> p h t f", h=HALVES), own,
                                         ACT.Relu, bias=bias_sb[:, 0:1]).then_inc(relu0_ready, 1)

            def relu_outer(k, g, j):
                if exists(g, GROUPS):
                    q = g * SLOTS + j
                    act.wait_ge(outer_ready[k], q + 1)
                    for i in range(QUAD):
                        x = outer[:, k, j % 2, i, :]
                        nc.scalar.activation(x, x, ACT.Relu, bias=bias_sb[:, k + 1:k + 2],
                                             accum_out=z_all[:, k + 1, bass.ds(q * QUAD + i, 1)]).then_inc(z_ready[k + 1], 1)

            def take_rep(k, g):
                if exists(g, GROUPS):
                    act.wait_ge(rep_done[k], g + 1)
                    at_least(act, outer_ready[k], g * SLOTS)
                    nc.scalar.copy(z_rep[:, k, :], rep_ps[:, 0:GROUP * F]).then_inc(rep_ready[k], 1)

            def step(g):
                for j in range(SLOTS):
                    relu_pairs(*before(g, j, 1))
                    take_turned(*before(g, j, -2))
                    if j == 3:
                        take_rep(0, g - 1)
                    if j == 1:
                        take_rep(1, g - 3)
                    relu_outer(0, *before(g, j, LAG1 + 1))
                    relu_outer(1, *before(g, j, LAG2 + 1))
                    if j == 2:
                        take_proj(g)

            take_turned(0, 0)
            take_turned(0, 1)
            for g in range(4):
                step(g)
            with act.Fori(4, GROUPS - 1) as g:
                step(g)
            for g in range(GROUPS - 1, LAST):
                step(g)

            act.wait_ge(top_in, N_TOP * 16)
            for c in range(CHUNKS):
                act.wait_ge(unpacked, c + 1)
                nc.scalar.copy(h0[0:LAYERS * F, c * CHUNK:(c + 1) * CHUNK], rep_ps[0:LAYERS * F, :]).then_inc(h0_ready, 1)
                for i in range(H1):
                    act.wait_ge(h1_done, c * H1 + i + 1)
                    if c > 0:
                        act.wait_ge(h2_done, c * H2)
                    nc.scalar.activation(h1[:, i, :], turn_ps[:, i // 2, i % 2 * 512:(i % 2 + 1) * 512], ACT.Relu,
                                         bias=b1_sb[:, i:i + 1]).then_inc(h1_ready, 1)
                for i in range(H2):
                    act.wait_ge(h2_done, c * H2 + i + 1)
                    if c > 0:
                        act.wait_ge(y_done, c)
                    nc.scalar.activation(h2[:, i, :], sum_ps[:, i, :], ACT.Relu, bias=b2_sb[:, i:i + 1]).then_inc(h2_ready, 1)
                act.wait_ge(y_done, c + 1)
                if c >= 2:
                    act.wait_ge(y_stored, 16 * (c - 1))
                nc.scalar.copy(y_sb[:, c % 2, :], proj_ps[0:1, :]).then_inc(y_ready, 1)

        @block.tensor
        def _(pe):
            pe.wait_ge(consts_in, N_CONSTS * 16)

            def turn(g, j):
                if exists(g, GROUPS):
                    q = g * SLOTS + j
                    pe.wait_ge(gathered[j], (g + 1) * QUAD * 16)
                    at_least(pe, emb_t_ready, 2 * (q - 1))
                    at_least(pe, prods_dve, made(*before(g, j, 2)))
                    for i in range(QUAD * EC):
                        last = nc.tensor.transpose(turn_ps[:, j % 2, i * P:(i + 1) * P], emb[:, j, i * P:(i + 1) * P], ident_sb[:])
                    last.then_inc(turned, 1)

            def sum_pairs(g, j):
                if exists(g, GROUPS):
                    q = g * SLOTS + j
                    pe.wait_ge(prods_dve, made(g, j))
                    if j in POOL_SLOTS:
                        pe.wait_ge(prods_pool, made_pool(g, j))
                    for h in range(HALVES):
                        at_least(pe, relu0_ready, RELUS0 * q)
                        x = prods[:, j % 2, h * PAIR_TILES:(h + 1) * PAIR_TILES, :]
                        x = x.rearrange("p t (c r k) -> p c r t k", c=EC, r=ROWS)
                        for c in range(EC):
                            for odd in range(2):
                                for s in range(ROWS // 2):
                                    last = nc.tensor.matmul(
                                        sum_ps[s * 2 * F:(s + 1) * 2 * F, h, 0:PAIR_TILES * PAIRS], w_sb[:, 0, c, odd, :],
                                        x[:, c, 2 * s + odd, :, :], start=c == 0 and odd == 0, stop=c == EC - 1 and odd == 1)
                        last.then_inc(sums_done, 1)

            def project(g):
                if exists(g, GROUPS):
                    pe.wait_ge(emb_t_ready, 2 * SLOTS * (g + 1))
                    at_least(pe, proj_ready, g)
                    x = emb_t[:].rearrange("p q (t c r w) -> p c r (q t) w", t=QUAD, c=EC, r=ROWS)
                    for k in range(2):
                        for c in range(EC):
                            for odd in range(2):
                                for s in range(ROWS // 2):
                                    last = nc.tensor.matmul(
                                        proj_ps[s * 2 * F:(s + 1) * 2 * F, k * GROUP * F:(k + 1) * GROUP * F],
                                        w_sb[:, k + 1, c, odd, :], x[:, c, 2 * s + odd, :, 0:F],
                                        start=c == 0 and odd == 0, stop=c == EC - 1 and odd == 1)
                    last.then_inc(proj_done, 1)

            def repeat_z(k, g):
                if exists(g, GROUPS):
                    pe.wait_ge(diag_ready[k], g + 1)
                    if k == 0:
                        at_least(pe, rep_ready[1], g - 1)
                    else:
                        pe.wait_ge(rep_ready[0], min(g + 2, GROUPS) if isinstance(g, int) else g + 2)
                    nc.tensor.matmul(rep_ps[:, 0:GROUP * F], ones_sb[:], z_diag[:, k, :], start=True, stop=True).then_inc(rep_done[k], 1)

            def step(g):
                for j in range(SLOTS):
                    turn(*before(g, j, -2))
                    if j == 1:
                        repeat_z(1, g - 3)
                    if j == 2:
                        repeat_z(0, g - 1)
                    sum_pairs(g, j)
                    if j == 1:
                        project(g)

            turn(0, 0)
            turn(0, 1)
            for g in range(4):
                step(g)
            with pe.Fori(4, GROUPS - 1) as g:
                step(g)
            for g in range(GROUPS - 1, LAST):
                step(g)

            pe.wait_ge(top_in, N_TOP * 16)
            pe.wait_ge(z_ready[2], TILES)
            pe.wait_ge(rep_ready[1], GROUPS)
            for c in range(CHUNKS):
                if c > 0:
                    pe.wait_ge(h0_ready, c)
                for r in range(ROWS):
                    for k in range(LAYERS):
                        last = nc.tensor.matmul(rep_ps[0:LAYERS * F, r * CHUNK_TILES:(r + 1) * CHUNK_TILES], unpack_sb[:, k, r, :],
                                                z_all[:, k, c * CHUNK_TILES:(c + 1) * CHUNK_TILES], start=k == 0, stop=k == LAYERS - 1)
                last.then_inc(unpacked, 1)
                pe.wait_ge(h0_ready, c + 1)
                for i in range(H1):
                    if c > 0:
                        pe.wait_ge(h1_ready, (c - 1) * H1 + i + 1)
                    nc.tensor.matmul(turn_ps[:, i // 2, i % 2 * 512:(i % 2 + 1) * 512], w1_sb[:, i * P:(i + 1) * P],
                                     h0[:, c * CHUNK:(c + 1) * CHUNK], start=True, stop=True).then_inc(h1_done, 1)
                for i in range(H2):
                    if c > 0:
                        pe.wait_ge(h2_ready, (c - 1) * H2 + i + 1)
                    for a in range(H1):
                        pe.wait_ge(h1_ready, c * H1 + a + 1)
                        last = nc.tensor.matmul(sum_ps[:, i, :], w2_sb[:, a, i * P:(i + 1) * P], h1[:, a, :],
                                                start=a == 0, stop=a == H1 - 1)
                    last.then_inc(h2_done, 1)
                if c > 0:
                    pe.wait_ge(y_ready, c)
                for i in range(H2):
                    pe.wait_ge(h2_ready, c * H2 + i + 1)
                    last = nc.tensor.matmul(proj_ps[0:1, :], w3_sb[:, i:i + 1], h2[:, i, :], start=i == 0, stop=i == H2 - 1)
                last.then_inc(y_done, 1)


def shape_constants():
    row_of = np.arange(P) // F
    unpack = np.zeros((ROWS, F, LAYERS, ROWS, LAYERS, F), np.float32)
    for r in range(ROWS):
        for k in range(LAYERS):
            unpack[r, range(F), k, r, k, range(F)] = 1.0
    return dict(
        id_top=np.tile(np.array(VOCABS, np.int32) - 1, ROWS).reshape(P, 1),
        id_base=np.tile(np.cumsum([0] + VOCABS[:-1]).astype(np.int32), ROWS).reshape(P, 1),
        ident=np.eye(P, dtype=np.float32), block_ones=(row_of[:, None] == row_of[None, :]).astype(np.float32),
        own_field=np.tile(np.eye(F, dtype=np.float32), (ROWS, 1)),
        unpack_sel=unpack.reshape(P, LAYERS, ROWS, LAYERS * F))


def kernel(**inputs):
    import concourse.bacc as bacc
    from concourse.bass_utils import run_bass_kernel_spmd

    x = {name: np.asarray(a) for name, a in inputs.items()}
    ids = x["ids"].reshape(ROWS, TILES, F).transpose(0, 2, 1).reshape(P, TILES)
    w = x["L0_rec_Ws"].reshape(LAYERS, F, EC, P).transpose(3, 0, 2, 1)
    w_cols = np.zeros((P, LAYERS, EC, 2, 2 * F), w.dtype)
    w_cols[:, :, :, 0, :F] = w
    w_cols[:, :, :, 1, F:] = w
    dense = x["dense_ctx"].reshape(ROWS, CHUNKS, CHUNK_TILES, DENSE).transpose(3, 1, 0, 2).reshape(DENSE, BATCH)
    const = shape_constants()
    arrays = {
        "tables": np.concatenate([x[f"tbl_{i}"] for i in range(F)], axis=0),
        "ids_t": ids, "id_top": const["id_top"], "id_base": const["id_base"],
        "w_cols": w_cols, "biases": np.tile(x["L0_rec_bs"].T, (ROWS, 1)),
        "ident": const["ident"], "block_ones": const["block_ones"], "own_field": const["own_field"],
        "unpack_sel": const["unpack_sel"], "dense_t": dense,
        "w_top1": x["W_top1"], "b_top1": x["b_top1"].reshape(H1, P).T,
        "w_top2": x["W_top2"].reshape(H1, P, HID2).transpose(1, 0, 2), "b_top2": x["b_top2"].reshape(H2, P).T,
        "w_top3": x["W_top3"].reshape(H2, P).T,
    }
    arrays = {name: np.ascontiguousarray(a) for name, a in arrays.items()}
    nc = bacc.Bacc("TRN2", target_bir_lowering=False, num_devices=1)
    args = [nc.dram_tensor(name, a.shape, mybir.dt.from_np(a.dtype), kind="ExternalInput").ap() for name, a in arrays.items()]
    y = nc.dram_tensor("y", (1, BATCH), FP32, kind="ExternalOutput").ap()
    build(nc, *args, y)
    r = run_bass_kernel_spmd(nc, [arrays], core_ids=[0])
    got = r.results[0]["y"].reshape(CHUNKS, ROWS, CHUNK_TILES)
    return got.transpose(1, 0, 2).reshape(BATCH, 1)
```

```python
from contextlib import ExitStack

import numpy as np

import concourse.bass as bass
from concourse import mybir

FP32 = mybir.dt.float32
INT32 = mybir.dt.int32
UINT32 = mybir.dt.uint32
ALU = mybir.AluOpType
ACT = mybir.ActivationFunctionType
AX = mybir.AxisListType

VOCABS = [1250, 12500, 1000, 12500, 1250, 1250, 12500, 12500, 1000, 12500, 1250, 12500, 1250, 12500, 1000, 1000]

P = 128
BATCH = 2048
F = 16
E = 256
LAYERS = 3
EC = E // P
ROWS = P // F
TILES = BATCH // ROWS
QUAD = 4
QUADS = TILES // QUAD
GROUP = 16
SLOTS = GROUP // QUAD
GROUPS = TILES // GROUP
BLOCKS = QUAD * EC * ROWS
WRAP = F + F // 2
SHIFTS = F // 2
PAIRS = SHIFTS * F + F // 2
PAIR_TILES = 2
HALVES = QUAD // PAIR_TILES
SQUARES_ACT = 60
LAG1 = SLOTS + 3
LAG2 = 3 * SLOTS + 2
DENSE = 16
HID1, HID2 = 512, 256
COLS = ROWS * GROUP
H1 = HID1 // P
H2 = HID2 // P
RELUS0 = QUAD + 1
POOL_BLOCKS = {q: 8 if q < LAG1 + 1 or q > QUADS - SLOTS else 4
               for q in [*range(1, LAG2 + 1), *range(QUADS - SLOTS + 1, QUADS)]}
VECTOR_QUADS = ((56, 58, 61), (49, 51, 53, 55, 57, 59, 60, 62))


def others(k, q):
    return q - len([v for v in VECTOR_QUADS[k] if v < q]) if isinstance(q, int) else q


def pool_blocks(g, j):
    return POOL_BLOCKS.get(g * SLOTS + j, 0) if isinstance(g, int) else 0


def on_vector(k, q):
    return isinstance(q, int) and q in VECTOR_QUADS[k]


def at_least(eng, sem, value):
    if not isinstance(value, int) or value > 0:
        eng.wait_ge(sem, value)


def through(n):
    return min(n, GROUPS) if isinstance(n, int) else n


def exists(n, count):
    return not isinstance(n, int) or 0 <= n < count


def build(nc, tables, ids_t, id_limits, w_cols, biases, ident, block_ones, own_field, ones,
          unpack_sel, dense_t, w_top1, b_top1, b_cols1, w_top2, b_top2, b_cols2, w_top3, y_out):
    ctx = ExitStack()
    with ctx:
        def sb(name, shape, dt=FP32):
            return ctx.enter_context(nc.sbuf_tensor(name, shape, dt))

        def ps(name, shape):
            return ctx.enter_context(nc.psum_tensor(name, shape, FP32))

        def sem(name):
            return ctx.enter_context(nc.semaphore(name))

        emb = sb("emb", [P, SLOTS, QUAD * E])
        emb_t = sb("emb_t", [P, SLOTS, BLOCKS * WRAP])
        prods = sb("prods", [P, 2, QUAD, EC * ROWS * PAIRS])
        relu0 = sb("relu0", [P, QUAD, PAIRS - F])
        own0 = sb("own0", [P, GROUP, F])
        own_sum0 = sb("own_sum0", [P, GROUP])
        proj = sb("proj", [P, TILES, 2, F])
        outer = sb("outer", [P, 2, 2, QUAD, F * F])
        z_all = sb("z_all", [P, LAYERS, TILES])
        z_diag = sb("z_diag", [P, 2, GROUP * F])
        z_rep = sb("z_rep", [P, 2, GROUP * F])
        ids_sb = sb("ids_sb", [P, TILES], INT32)
        rows_sb = sb("rows_sb", [P, TILES], INT32)
        rows_now = sb("rows_now", [P, GROUP], UINT32)
        id_lim = sb("id_lim", [P, 2], INT32)
        id_lim_f = sb("id_lim_f", [P, 2])
        w_sb = sb("w_sb", [P, LAYERS, EC, 2, 2 * F])
        bias_sb = sb("bias_sb", [P, LAYERS])
        ident_sb = sb("ident_sb", [P, P])
        ones_sb = sb("ones_sb", [P, P])
        own_sb = sb("own_sb", [P, F])
        unpack_sb = sb("unpack_sb", [P, LAYERS, ROWS, LAYERS * F])
        h0 = sb("h0", [LAYERS * F + DENSE, BATCH])
        w1_sb = sb("w1_sb", [LAYERS * F + DENSE, HID1])
        w2_sb = sb("w2_sb", [P, H1, HID2])
        w3_sb = sb("w3_sb", [P, H2])
        b_cols = sb("b_cols", [P, H1 + H2])
        b_rows = sb("b_rows", [1, HID1 + HID2])
        one_row = sb("one_row", [1, COLS])
        h1 = sb("h1", [P, H1 * COLS])
        h2 = sb("h2", [P, H2 * COLS])
        y_sb = sb("y_sb", [1, BATCH])

        turn_ps = ps("turn_ps", [P, 2, QUAD * E])
        sum_ps = ps("sum_ps", [P, HALVES, 512])
        proj_ps = ps("proj_ps", [P, 512])
        rep_ps = ps("rep_ps", [P, 512])

        ids_in = sem("ids_in")
        consts_in = sem("consts_in")
        top_in = sem("top_in")
        dve_setup = sem("dve_setup")
        rows_ready = sem("rows_ready")
        rows_copied = sem("rows_copied")
        gathered = [sem(f"gathered{j}") for j in range(SLOTS)]
        turned = sem("turned")
        emb_t_ready = sem("emb_t_ready")
        prods_dve = sem("prods_dve")
        squares_ready = sem("squares_ready")
        squares_pool = sem("squares_pool")
        prods_pool = sem("prods_pool")
        sums_done = sem("sums_done")
        relu0_ready = sem("relu0_ready")
        own_sum_ready = sem("own_sum_ready")
        proj_done = sem("proj_done")
        proj_ready = sem("proj_ready")
        z0_ready = sem("z0_ready")
        z_ready = [None, sem("z_ready1"), sem("z_ready2")]
        diag_ready = [sem(f"diag_ready{k}") for k in range(2)]
        rep_done = [sem(f"rep_done{k}") for k in range(2)]
        rep_ready = [sem(f"rep_ready{k}") for k in range(2)]
        outer_ready = [sem(f"outer_ready{k}") for k in range(2)]
        outer_vector = [sem(f"outer_vector{k}") for k in range(2)]
        relu_vector = [sem(f"relu_vector{k}") for k in range(2)]
        z_vector = [sem(f"z_vector{k}") for k in range(2)]
        unpacked = sem("unpacked")
        h0_ready = sem("h0_ready")
        h1_done = sem("h1_done")
        h1_ready = sem("h1_ready")
        h2_done = sem("h2_done")
        h2_ready = sem("h2_ready")
        y_done = sem("y_done")
        y_ready = sem("y_ready")
        y_stored = sem("y_stored")

        N_CONSTS = 5
        N_TOP = 10
        LAST = GROUPS - 1
        TOP_GROUPS = GROUPS - 4
        LOOP_FROM = 6

        def made(g, j):
            return 2 * (g * SLOTS + j + 1)

        def made_pool(g, j):
            return 2 * len([q for q in POOL_BLOCKS if q <= g * SLOTS + j])

        def before(g, j, by):
            return g + (j - by) // SLOTS, (j - by) % SLOTS

        def multiply(eng, j, b0, b1, own, done):
            x = emb_t[:, j, :].rearrange("p (n w) -> p n w", w=WRAP)[:, b0:b1, :]
            out = prods[:, j % 2, :, :].rearrange("p t (n k) -> p (t n) k", k=PAIRS)[:, b0:b1, :]
            step = [list(d) for d in x.ap]
            shifted = bass.AP(x.tensor, x.offset + 1, [step[0], step[1], [1, SHIFTS - 1], [1, F]])
            same = own[:, b0:b1, :]
            every = same[:, :, 0:F].rearrange("p n (u f) -> p n u f", u=1).broadcast_to([P, b1 - b0, SHIFTS - 1, F])
            eng.tensor_tensor(out[:, :, F:SHIFTS * F].rearrange("p n (s f) -> p n s f", f=F), every, shifted,
                              ALU.mult).then_inc(done, 1)
            eng.tensor_tensor(out[:, :, SHIFTS * F:], same[:, :, 0:F // 2], x[:, :, F // 2:F], ALU.mult).then_inc(done, 1)

        def quad_waits(eng, g, j):
            eng.wait_ge(emb_t_ready, 2 * (g * SLOTS + j + 1))
            at_least(eng, sums_done, HALVES * (g * SLOTS + j - 1))

        def outer_product(eng, k, g, j, out, done):
            q = g * SLOTS + j
            y = proj[:, bass.ds(q * QUAD, QUAD), k, :]
            y = y.rearrange("p t (f u) -> p t f u", u=1).broadcast_to([P, QUAD, F, F])
            z = z_rep[:, k, j * QUAD * F:(j + 1) * QUAD * F].rearrange("p (t u f) -> p t u f", u=1, f=F)
            z = z.broadcast_to([P, QUAD, F, F])
            eng.tensor_tensor(out.rearrange("p t (f g) -> p t f g", g=F), y, z, ALU.mult).then_inc(done, 1)

        def spread(eng, k, g):
            if exists(g, GROUPS):
                if k == 0:
                    eng.wait_ge(z0_ready, g + 1)
                else:
                    eng.wait_ge(z_ready[1], others(0, (g + 1) * SLOTS) * QUAD)
                    if isinstance(g, int):
                        at_least(eng, z_vector[0], (g + 1) * SLOTS - others(0, (g + 1) * SLOTS))
                at_least(eng, rep_ready[k], g)
                z = z_all[:, k, bass.ds(g * GROUP, GROUP)].rearrange("p (t u) -> p t u", u=1).broadcast_to([P, GROUP, F])
                m = own_sb[:].rearrange("p (u f) -> p u f", u=1).broadcast_to([P, GROUP, F])
                eng.tensor_tensor(z_diag[:, k, :].rearrange("p (t f) -> p t f", f=F), z, m, ALU.mult).then_inc(diag_ready[k], 1)

        def by_row(x, g, groups=1):
            return x.rearrange("p (r t) -> p r t", r=ROWS)[:, :, bass.ds(g * GROUP, groups * GROUP)]

        PAIR_COLS = 2 * COLS
        pair_h1 = prods[:, 1, 0, 0:H1 * PAIR_COLS]
        pair_h2 = prods[:, 1, 1, 0:H2 * PAIR_COLS]
        pair_first_ps = turn_ps[0:2 * F, 1, 0:PAIR_COLS]
        pair_last_ps = turn_ps[2 * F:LAYERS * F, 1, 512:512 + PAIR_COLS]
        pair_h1_ps = [turn_ps[:, 0, 0:PAIR_COLS], turn_ps[:, 0, 512:512 + PAIR_COLS],
                      sum_ps[:, 0, 0:PAIR_COLS], sum_ps[:, 1, 0:PAIR_COLS]]
        pair_h2_ps = pair_h1_ps[0:H2]
        pair_y_ps = proj_ps[0:1, 0:PAIR_COLS]

        block = ctx.enter_context(nc.Block())

        @block.sync
        def _(sp):
            sp.dma_start(ids_sb[:], ids_t).then_inc(ids_in, 16)
            sp.dma_start(id_lim[:], id_limits).then_inc(ids_in, 16)
            sp.dma_start(ident_sb[:], ident).then_inc(consts_in, 16)
            sp.dma_start(w_sb[:], w_cols).then_inc(consts_in, 16)
            sp.dma_start(bias_sb[:], biases).then_inc(consts_in, 16)
            sp.dma_start(ones_sb[:], block_ones).then_inc(consts_in, 16)
            sp.dma_start(own_sb[:], own_field).then_inc(consts_in, 16)
            sp.wait_ge(gathered[0], QUAD * 16)
            sp.dma_start(unpack_sb[:], unpack_sel).then_inc(top_in, 16)
            sp.dma_start(h0[LAYERS * F:, :], dense_t).then_inc(top_in, 16)
            sp.dma_start(w1_sb[:], w_top1).then_inc(top_in, 16)
            sp.dma_start(b_rows[:, 0:HID1], b_top1).then_inc(top_in, 16)
            sp.dma_start(w2_sb[:], w_top2).then_inc(top_in, 16)
            sp.dma_start(b_rows[:, HID1:], b_top2).then_inc(top_in, 16)
            sp.dma_start(w3_sb[:], w_top3).then_inc(top_in, 16)
            sp.dma_start(b_cols[:, 0:H1], b_cols1).then_inc(top_in, 16)
            sp.dma_start(b_cols[:, H1:], b_cols2).then_inc(top_in, 16)
            sp.dma_start(one_row[:], ones).then_inc(top_in, 16)
            sp.wait_ge(y_ready, TOP_GROUPS + 2)
            sp.dma_start(y_out, y_sb[:]).then_inc(y_stored, 16)
            sp.wait_ge(y_stored, 16)

        @block.gpsimd
        def _(pool):
            pool.wait_ge(rows_ready, 1)

            def take_rows(g):
                if exists(g, GROUPS):
                    for j in range(SLOTS):
                        at_least(pool, gathered[j], g * QUAD * 16)
                    nc.gpsimd.tensor_copy(rows_now[:], rows_sb[:, bass.ds(g * GROUP, GROUP)].bitcast(UINT32)).then_inc(rows_copied, 1)

            def may_gather(g, j):
                if exists(g, GROUPS):
                    pool.wait_ge(rows_copied, g + 1)
                    at_least(pool, turned, (g - 1) * SLOTS + j + 1)

            def gather(g, j):
                if exists(g, GROUPS):
                    for i in range(QUAD):
                        nc.gpsimd.indirect_dma_start(
                            out=emb[:, j, i * E:(i + 1) * E], out_offset=None, in_=tables,
                            in_offset=bass.IndirectOffsetOnAxis(ap=rows_now[:, j * QUAD + i:j * QUAD + i + 1], axis=0),
                        ).then_inc(gathered[j], 16)

            def products(g, j):
                if exists(g, GROUPS):
                    quad_waits(pool, g, j)
                    x = emb_t[:, j, :].rearrange("p (n w) -> p n w", w=WRAP)[:, SQUARES_ACT:, 0:F]
                    out = prods[:, j % 2, :, :].rearrange("p t (n k) -> p (t n) k", k=PAIRS)[:, SQUARES_ACT:, 0:F]
                    nc.gpsimd.tensor_tensor(out, x, x, ALU.mult).then_inc(squares_pool, 1)
                if exists(g, GROUPS) and pool_blocks(g, j):
                    multiply(nc.gpsimd, j, BLOCKS - pool_blocks(g, j), BLOCKS, emb_t[:, j, :].rearrange("p (n w) -> p n w", w=WRAP), prods_pool)

            def outer_products(k, g, j):
                if exists(g, GROUPS) and not on_vector(k, g * SLOTS + j):
                    n = others(k, g * SLOTS + j)
                    pool.wait_ge(rep_ready[k], g + 1)
                    at_least(pool, z_ready[k + 1], QUAD * (n - 1))
                    outer_product(nc.gpsimd, k, g, j, outer[:, k, (n if isinstance(n, int) else j) % 2, :, :], outer_ready[k])

            def step(g):
                for j in range(SLOTS):
                    if j == 0:
                        take_rows(g + 1)
                    may_gather(g + 1, j)
                    g1, j1 = before(g, j, -1)
                    products(g1, j1)
                    outer_products(1, *before(g, j, LAG2))
                    gather(g + 1, j)
                    outer_products(0, *before(g, j, LAG1))
                    if j == 0:
                        spread(nc.gpsimd, 1, g - 3)

            take_rows(0)
            may_gather(0, 0)
            for j in range(SLOTS):
                gather(0, j)
            pool.wait_ge(consts_in, N_CONSTS * 16)
            products(0, 0)
            for g in range(LOOP_FROM):
                step(g)
            with pool.Fori(LOOP_FROM, GROUPS - 1) as g:
                step(g)
            step(LAST)
            for k, q in ((0, 57), (1, 50), (0, 59), (1, 52), (0, 60), (1, 54), (0, 62), (0, 63),
                         (1, 56), (1, 58), (1, 61), (1, 63)):
                outer_products(k, *divmod(q, SLOTS))

        @block.vector
        def _(dve):
            dve.wait_ge(ids_in, 2 * 16)
            nc.vector.tensor_copy(id_lim_f[:], id_lim[:]).then_inc(dve_setup, 1)
            dve.wait_ge(dve_setup, 1)
            nc.vector.tensor_scalar(rows_sb[:], ids_sb[:], 0.0, id_lim_f[:, 0:1], ALU.max, ALU.min).then_inc(dve_setup, 1)
            dve.wait_ge(dve_setup, 2)
            nc.vector.tensor_scalar(rows_sb[:], rows_sb[:], id_lim_f[:, 1:2], None, ALU.add).then_inc(rows_ready, 1)
            dve.wait_ge(consts_in, N_CONSTS * 16)

            def finish0(g):
                if exists(g, GROUPS):
                    dve.wait_ge(relu0_ready, RELUS0 * SLOTS * (g + 1))
                    nc.vector.tensor_reduce(own_sum0[:], own0[:], AX.X, ALU.add).then_inc(own_sum_ready, 1)
                    dve.wait_ge(own_sum_ready, g + 1)
                    z = z_all[:, 0, bass.ds(g * GROUP, GROUP)]
                    nc.vector.scalar_tensor_tensor(out=z, in0=z, scalar=2.0, in1=own_sum0[:],
                                                   op0=ALU.mult, op1=ALU.add).then_inc(z0_ready, 1)

            def products(g, j):
                if exists(g, GROUPS):
                    quad_waits(dve, g, j)
                    multiply(nc.vector, j, 0, BLOCKS - pool_blocks(g, j), turn_ps[:, j % 2, :].rearrange("p (n f) -> p n f", f=F), prods_dve)

            def whole_quad(k, q):
                g, j = divmod(q, SLOTS)
                n = VECTOR_QUADS[k].index(q) + 1
                x = prods[:, 0, 2 * k + n % 2, 0:QUAD * F * F].rearrange("p (t n) -> p t n", t=QUAD)
                dve.wait_ge(sums_done, HALVES * (QUADS - 1))
                dve.wait_ge(rep_ready[k], g + 1)
                outer_product(nc.vector, k, g, j, x, outer_vector[k])
                dve.wait_ge(outer_vector[k], n)
                nc.vector.tensor_scalar(x, x, bias_sb[:, k + 1:k + 2], 0.0, ALU.add, ALU.max).then_inc(relu_vector[k], 1)
                dve.wait_ge(relu_vector[k], n)
                nc.vector.tensor_reduce(z_all[:, k + 1, q * QUAD:(q + 1) * QUAD], x, AX.X, ALU.add).then_inc(z_vector[k], 1)

            def step(g):
                for j in range(SLOTS):
                    products(*before(g, j, -1))
                    if j == 0:
                        finish0(g - 1)
                    if j == 1:
                        spread(nc.vector, 0, g - 1)

            products(0, 0)
            for g in range(LOOP_FROM):
                step(g)
            with dve.Fori(LOOP_FROM, GROUPS - 1) as g:
                step(g)
            step(LAST)
            whole_quad(1, 49)
            whole_quad(0, 56)
            spread(nc.vector, 1, LAST - 2)
            finish0(LAST)
            spread(nc.vector, 0, LAST)
            whole_quad(0, 58)
            whole_quad(1, 51)
            whole_quad(1, 53)
            spread(nc.vector, 1, LAST - 1)
            whole_quad(1, 55)
            whole_quad(0, 61)
            whole_quad(1, 57)
            spread(nc.vector, 1, LAST)
            whole_quad(1, 59)
            whole_quad(1, 60)
            whole_quad(1, 62)

        @block.scalar
        def _(act):
            act.wait_ge(consts_in, N_CONSTS * 16)
            nc.scalar.activation(h1[:, 0:LAYERS], bias_sb[:], ACT.Relu)

            def take_turned(g, j):
                if exists(g, GROUPS):
                    q = g * SLOTS + j
                    act.wait_ge(turned, q + 1)
                    at_least(act, prods_dve, made(g - 1, j))
                    if pool_blocks(g - 1, j):
                        at_least(act, prods_pool, made_pool(g - 1, j))
                    at_least(act, proj_done, 2 * g - 1 + j // 2)
                    at_least(act, squares_pool, (g - 1) * SLOTS + j + 1)
                    src = turn_ps[:, j % 2, :].rearrange("p (n f) -> p n f", f=F)
                    out = emb_t[:, j, :].rearrange("p (n w) -> p n w", w=WRAP)
                    nc.scalar.copy(out[:, :, 0:F], src).then_inc(emb_t_ready, 1)
                    nc.scalar.copy(out[:, :, F:WRAP], src[:, :, 0:F // 2]).then_inc(emb_t_ready, 1)

            def squares(g, j):
                if exists(g, GROUPS):
                    q = g * SLOTS + j
                    act.wait_ge(emb_t_ready, 2 * (q + 1))
                    at_least(act, sums_done, HALVES * (q - 1))
                    out = prods[:, j % 2, :, :].rearrange("p t (n k) -> p (t n) k", k=PAIRS)[:, 0:SQUARES_ACT, 0:F]
                    nc.scalar.square(out, emb_t[:, j, :].rearrange("p (n w) -> p n w", w=WRAP)[:, 0:SQUARES_ACT, 0:F]).then_inc(squares_ready, 1)

            def take_proj(g):
                if exists(g, GROUPS):
                    act.wait_ge(proj_done, 2 * g + 2)
                    nc.scalar.copy(proj[:, bass.ds(g * GROUP, GROUP), :, :],
                                   proj_ps[:].rearrange("p (k t f) -> p t k f", k=2, f=F)).then_inc(proj_ready, 1)

            def relu_pairs(g, j):
                if exists(g, GROUPS):
                    q = g * SLOTS + j
                    for i in range(QUAD):
                        h, t = i // PAIR_TILES, i % PAIR_TILES
                        act.wait_ge(sums_done, HALVES * q + h + 1)
                        nc.scalar.activation(relu0[:, i, :], sum_ps[:, h, t * PAIRS + F:(t + 1) * PAIRS], ACT.Relu,
                                             bias=bias_sb[:, 0:1], accum_out=z_all[:, 0, bass.ds(q * QUAD + i, 1)]).then_inc(relu0_ready, 1)
                    at_least(act, own_sum_ready, g)
                    own = sum_ps[:, :, 0:PAIR_TILES * PAIRS].rearrange("p h (t k) -> p h t k", k=PAIRS)[:, :, :, 0:F]
                    nc.scalar.activation(own0[:, j * QUAD:(j + 1) * QUAD, :].rearrange("p (h t) f -> p h t f", h=HALVES), own,
                                         ACT.Relu, bias=bias_sb[:, 0:1]).then_inc(relu0_ready, 1)

            def relu_outer(k, g, j):
                if exists(g, GROUPS) and not on_vector(k, g * SLOTS + j):
                    q = g * SLOTS + j
                    n = others(k, q)
                    act.wait_ge(outer_ready[k], n + 1)
                    for i in range(QUAD):
                        x = outer[:, k, (n if isinstance(n, int) else j) % 2, i, :]
                        nc.scalar.activation(x, x, ACT.Relu, bias=bias_sb[:, k + 1:k + 2],
                                             accum_out=z_all[:, k + 1, bass.ds(q * QUAD + i, 1)]).then_inc(z_ready[k + 1], 1)

            def take_rep(k, g):
                if exists(g, GROUPS):
                    act.wait_ge(rep_done[k], g + 1)
                    at_least(act, outer_ready[k], others(k, g * SLOTS))
                    if isinstance(g, int):
                        at_least(act, outer_vector[k], g * SLOTS - others(k, g * SLOTS))
                    nc.scalar.copy(z_rep[:, k, :], rep_ps[:, 0:GROUP * F]).then_inc(rep_ready[k], 1)

            def step(g):
                for j in range(SLOTS):
                    relu_pairs(*before(g, j, 1))
                    if j == 2:
                        take_rep(1, g - 3)
                    relu_outer(0, *before(g, j, LAG1 + 1))
                    if j == 0:
                        take_unpacked(g - 5)
                        relu_hidden2(g - 6)
                    if j == 1:
                        take_output(g - 6)
                        relu_hidden1(g - 5)
                    if j == 3:
                        take_proj(g)
                        take_rep(0, g - 1)
                    take_turned(*before(g, j, -2))
                    squares(*before(g, j, -1))
                    relu_outer(1, *before(g, j, LAG2 + 1))

            def take_unpacked(g):
                if exists(g, GROUPS):
                    act.wait_ge(unpacked, g + 1)
                    nc.scalar.copy(by_row(h0[0:LAYERS * F, :], g),
                                   rep_ps[0:LAYERS * F, 0:COLS].rearrange("p (r t) -> p r t", r=ROWS)).then_inc(h0_ready, 1)

            def relu_hidden1(g):
                if exists(g, GROUPS):
                    act.wait_ge(h1_done, g + 1)
                    nc.scalar.activation(h1[:], proj_ps[:, 0:H1 * COLS], ACT.Relu).then_inc(h1_ready, 1)

            def relu_hidden2(g):
                if exists(g, GROUPS):
                    act.wait_ge(h2_done, g + 1)
                    nc.scalar.activation(h2[:], proj_ps[:, 0:H2 * COLS], ACT.Relu).then_inc(h2_ready, 1)

            def take_output(g):
                if exists(g, GROUPS):
                    act.wait_ge(y_done, g + 1)
                    nc.scalar.copy(by_row(y_sb[:], g), rep_ps[0:1, 0:COLS].rearrange("p (r t) -> p r t", r=ROWS)).then_inc(y_ready, 1)

            take_turned(0, 0)
            take_turned(0, 1)
            squares(0, 0)
            step(0)
            act.wait_ge(top_in, N_TOP * 16)
            for g in range(1, LOOP_FROM):
                step(g)
            with act.Fori(LOOP_FROM, GROUPS - 1) as g:
                step(g)
            step(LAST)

            def pair_features(n, first):
                act.wait_ge(unpacked, TOP_GROUPS + 2 * n + (1 if first else 2))
                rows, src = (slice(0, 2 * F), pair_first_ps) if first else (slice(2 * F, LAYERS * F), pair_last_ps)
                nc.scalar.copy(by_row(h0[rows, :], TOP_GROUPS + 2 * n, 2),
                               src.rearrange("p (r t) -> p r t", r=ROWS)).then_inc(h0_ready, 1)

            def pair_hidden1(n):
                for i in range(H1):
                    act.wait_ge(h1_done, TOP_GROUPS + H1 * n + i + 1)
                    cols = slice(i * PAIR_COLS, (i + 1) * PAIR_COLS)
                    nc.scalar.activation(pair_h1[:, cols], pair_h1_ps[i], ACT.Relu,
                                         bias=b_cols[:, i:i + 1]).then_inc(h1_ready, 1)

            def pair_hidden2(n):
                for i in range(H2):
                    act.wait_ge(h2_done, TOP_GROUPS + H2 * n + i + 1)
                    nc.scalar.activation(pair_h2[:, i * PAIR_COLS:(i + 1) * PAIR_COLS], pair_h2_ps[i], ACT.Relu,
                                         bias=b_cols[:, H1 + i:H1 + i + 1]).then_inc(h2_ready, 1)

            def pair_output(n):
                act.wait_ge(y_done, TOP_GROUPS + n + 1)
                nc.scalar.copy(by_row(y_sb[:], TOP_GROUPS + 2 * n, 2),
                               pair_y_ps.rearrange("p (r t) -> p r t", r=ROWS)).then_inc(y_ready, 1)

            def layer(k, q):
                relu_outer(k, *divmod(q, SLOTS))

            relu_pairs(LAST, SLOTS - 1)
            take_unpacked(LAST - 4)
            relu_hidden2(LAST - 5)
            layer(0, 57)
            take_output(LAST - 5)
            take_rep(1, LAST - 2)
            layer(0, 59)
            take_rep(0, LAST)
            layer(1, 50)
            relu_hidden1(LAST - 4)
            layer(0, 60)
            take_rep(1, LAST - 1)
            layer(1, 52)
            relu_hidden2(LAST - 4)
            layer(0, 62)
            take_output(LAST - 4)
            layer(0, 63)
            layer(1, 54)
            layer(1, 56)
            pair_features(0, True)
            pair_features(0, False)
            take_rep(1, LAST)
            layer(1, 58)
            pair_hidden1(0)
            layer(1, 61)
            pair_hidden2(0)
            layer(1, 63)
            pair_output(0)
            pair_features(1, True)
            pair_features(1, False)
            pair_hidden1(1)
            pair_hidden2(1)
            pair_output(1)

        @block.tensor
        def _(pe):
            pe.wait_ge(consts_in, N_CONSTS * 16)

            def turn(g, j):
                if exists(g, GROUPS):
                    q = g * SLOTS + j
                    pe.wait_ge(gathered[j], (g + 1) * QUAD * 16)
                    at_least(pe, emb_t_ready, 2 * (q - 1))
                    at_least(pe, prods_dve, made(*before(g, j, 2)))
                    for i in range(QUAD * EC):
                        last = nc.tensor.transpose(turn_ps[:, j % 2, i * P:(i + 1) * P], emb[:, j, i * P:(i + 1) * P], ident_sb[:])
                    last.then_inc(turned, 1)

            def sum_pairs(g, j):
                if exists(g, GROUPS):
                    q = g * SLOTS + j
                    pe.wait_ge(squares_ready, q + 1)
                    pe.wait_ge(squares_pool, q + 1)
                    pe.wait_ge(prods_dve, made(g, j))
                    if pool_blocks(g, j):
                        pe.wait_ge(prods_pool, made_pool(g, j))
                    for h in range(HALVES):
                        at_least(pe, relu0_ready, RELUS0 * q)
                        x = prods[:, j % 2, h * PAIR_TILES:(h + 1) * PAIR_TILES, :]
                        x = x.rearrange("p t (c r k) -> p c r t k", c=EC, r=ROWS)
                        for c in range(EC):
                            for odd in range(2):
                                for s in range(ROWS // 2):
                                    last = nc.tensor.matmul(
                                        sum_ps[s * 2 * F:(s + 1) * 2 * F, h, 0:PAIR_TILES * PAIRS], w_sb[:, 0, c, odd, :],
                                        x[:, c, 2 * s + odd, :, :], start=c == 0 and odd == 0, stop=c == EC - 1 and odd == 1)
                        last.then_inc(sums_done, 1)

            def project(g, half):
                if exists(g, GROUPS):
                    quads = SLOTS // 2
                    cols = quads * QUAD * F
                    pe.wait_ge(emb_t_ready, 2 * (g * SLOTS + (half + 1) * quads))
                    at_least(pe, proj_ready, g)
                    at_least(pe, h1_ready, g - 4)
                    x = emb_t[:, half * quads:(half + 1) * quads, :].rearrange("p q (t c r w) -> p c r (q t) w", t=QUAD, c=EC, r=ROWS)
                    for k in range(2):
                        out = proj_ps[:, (2 * k + half) * cols:(2 * k + half + 1) * cols]
                        for c in range(EC):
                            for odd in range(2):
                                for s in range(ROWS // 2):
                                    last = nc.tensor.matmul(out[s * 2 * F:(s + 1) * 2 * F, :], w_sb[:, k + 1, c, odd, :],
                                                            x[:, c, 2 * s + odd, :, 0:F],
                                                            start=c == 0 and odd == 0, stop=c == EC - 1 and odd == 1)
                    last.then_inc(proj_done, 1)

            def repeat_z(k, g):
                if exists(g, GROUPS):
                    pe.wait_ge(diag_ready[k], g + 1)
                    if k == 0:
                        at_least(pe, rep_ready[1], g - 1)
                    else:
                        pe.wait_ge(rep_ready[0], through(g + 2))
                        at_least(pe, y_ready, min(g - 2, TOP_GROUPS - 1) if isinstance(g, int) else g - 2)
                    nc.tensor.matmul(rep_ps[:, 0:GROUP * F], ones_sb[:], z_diag[:, k, :], start=True, stop=True).then_inc(rep_done[k], 1)

            def step(g):
                for j in range(SLOTS):
                    turn(*before(g, j, -2))
                    sum_pairs(g, j)
                    if j == 1:
                        repeat_z(1, g - 3)
                        project(g, 0)
                    if j == 2:
                        repeat_z(0, g - 1)
                        project(g, 1)
                    if j == 3:
                        unpack(g - 4)
                        hidden2(g - 5)
                    if j == 0:
                        output(g - 6)
                        hidden1(g - 5)

            def unpack(g):
                if exists(g, GROUPS):
                    for k in range(1, LAYERS):
                        quads = others(k - 1, (g + 1) * SLOTS)
                        pe.wait_ge(z_ready[k], quads * QUAD)
                        if isinstance(g, int):
                            at_least(pe, z_vector[k - 1], (g + 1) * SLOTS - quads)
                    pe.wait_ge(rep_ready[0], through(g + 4))
                    pe.wait_ge(rep_ready[1], through(g + 2))
                    for r in range(ROWS):
                        for k in range(LAYERS):
                            last = nc.tensor.matmul(rep_ps[0:LAYERS * F, r * GROUP:(r + 1) * GROUP], unpack_sb[:, k, r, :],
                                                    z_all[:, k, bass.ds(g * GROUP, GROUP)], start=k == 0, stop=k == LAYERS - 1)
                    last.then_inc(unpacked, 1)

            def hidden1(g):
                if exists(g, GROUPS):
                    pe.wait_ge(h0_ready, g + 1)
                    at_least(pe, h2_ready, g)
                    for i in range(H1):
                        out = proj_ps[:, i * COLS:(i + 1) * COLS]
                        nc.tensor.matmul(out, w1_sb[:, i * P:(i + 1) * P], by_row(h0[:], g), start=True, stop=False)
                        last = nc.tensor.matmul(out, b_rows[:, i * P:(i + 1) * P], one_row[:], start=False, stop=True)
                    last.then_inc(h1_done, 1)

            def hidden2(g):
                if exists(g, GROUPS):
                    pe.wait_ge(h1_ready, g + 1)
                    pe.wait_ge(proj_ready, through(g + 6))
                    for i in range(H2):
                        out = proj_ps[:, i * COLS:(i + 1) * COLS]
                        for a in range(H1):
                            nc.tensor.matmul(out, w2_sb[:, a, i * P:(i + 1) * P], h1[:, a * COLS:(a + 1) * COLS],
                                             start=a == 0, stop=False)
                        last = nc.tensor.matmul(out, b_rows[:, HID1 + i * P:HID1 + (i + 1) * P], one_row[:], start=False, stop=True)
                    last.then_inc(h2_done, 1)

            def output(g, ahead=2):
                if exists(g, GROUPS):
                    pe.wait_ge(h2_ready, g + 1)
                    pe.wait_ge(h0_ready, through(g + ahead))
                    for i in range(H2):
                        last = nc.tensor.matmul(rep_ps[0:1, 0:COLS], w3_sb[:, i:i + 1], h2[:, i * COLS:(i + 1) * COLS],
                                                start=i == 0, stop=i == H2 - 1)
                    last.then_inc(y_done, 1)

            turn(0, 0)
            turn(0, 1)
            step(0)
            pe.wait_ge(top_in, N_TOP * 16)
            for g in range(1, LOOP_FROM):
                step(g)
            with pe.Fori(LOOP_FROM, GROUPS - 1) as g:
                step(g)
            step(LAST)

            def pair_features(n, first):
                pe.wait_ge(emb_t_ready, 2 * QUADS)
                pe.wait_ge(h0_ready, TOP_GROUPS + 2 * n)
                g = TOP_GROUPS + 2 * n
                layers = (0, 1) if first else (2,)
                out, cols = (pair_first_ps, slice(0, 2 * F)) if first else (pair_last_ps, slice(2 * F, LAYERS * F))
                quads = others(layers[-1] - 1, (g + 2) * SLOTS)
                pe.wait_ge(z_ready[layers[-1]], quads * QUAD)
                at_least(pe, z_vector[layers[-1] - 1], (g + 2) * SLOTS - quads)
                for r in range(ROWS):
                    for k in layers:
                        last = nc.tensor.matmul(out[:, r * 2 * GROUP:(r + 1) * 2 * GROUP], unpack_sb[:, k, r, cols],
                                                z_all[:, k, g * GROUP:(g + 2) * GROUP], start=k == layers[0], stop=k == layers[-1])
                last.then_inc(unpacked, 1)

            def pair_top(n):
                pe.wait_ge(relu0_ready, RELUS0 * QUADS)
                pe.wait_ge(proj_ready, GROUPS)
                pe.wait_ge(y_ready, TOP_GROUPS + n)
                pe.wait_ge(h0_ready, TOP_GROUPS + 2 * n + 2)
                for i in range(H1):
                    nc.tensor.matmul(pair_h1_ps[i], w1_sb[:, i * P:(i + 1) * P],
                                     by_row(h0[:], TOP_GROUPS + 2 * n, 2), start=True, stop=True).then_inc(h1_done, 1)
                for i in range(H2):
                    for a in range(H1):
                        pe.wait_ge(h1_ready, TOP_GROUPS + H1 * n + a + 1)
                        last = nc.tensor.matmul(pair_h2_ps[i], w2_sb[:, a, i * P:(i + 1) * P],
                                                pair_h1[:, a * PAIR_COLS:(a + 1) * PAIR_COLS], start=a == 0, stop=a == H1 - 1)
                    last.then_inc(h2_done, 1)
                for i in range(H2):
                    pe.wait_ge(h2_ready, TOP_GROUPS + H2 * n + i + 1)
                    last = nc.tensor.matmul(pair_y_ps, w3_sb[:, i:i + 1], pair_h2[:, i * PAIR_COLS:(i + 1) * PAIR_COLS],
                                            start=i == 0, stop=i == H2 - 1)
                last.then_inc(y_done, 1)

            output(LAST - 5)
            repeat_z(1, LAST - 2)
            repeat_z(0, LAST)
            hidden1(LAST - 4)
            repeat_z(1, LAST - 1)
            hidden2(LAST - 4)
            pe.wait_ge(rep_ready[1], LAST)
            output(LAST - 4, 1)
            pair_features(0, True)
            pair_features(0, False)
            pe.wait_ge(y_ready, TOP_GROUPS)
            repeat_z(1, LAST)
            pair_top(0)
            pair_features(1, True)
            pair_features(1, False)
            pair_top(1)


def shape_constants():
    row_of = np.arange(P) // F
    unpack = np.zeros((ROWS, F, LAYERS, ROWS, LAYERS, F), np.float32)
    for r in range(ROWS):
        for k in range(LAYERS):
            unpack[r, range(F), k, r, k, range(F)] = 1.0
    return dict(
        id_limits=np.tile(np.stack([np.array(VOCABS) - 1, np.cumsum([0] + VOCABS[:-1])], axis=1).astype(np.int32), (ROWS, 1)),
        ident=np.eye(P, dtype=np.float32), block_ones=(row_of[:, None] == row_of[None, :]).astype(np.float32),
        ones=np.ones((1, COLS), np.float32), own_field=np.tile(np.eye(F, dtype=np.float32), (ROWS, 1)),
        unpack_sel=unpack.reshape(P, LAYERS, ROWS, LAYERS * F))


def kernel(**inputs):
    import concourse.bacc as bacc
    from concourse.bass_utils import run_bass_kernel_spmd

    x = {name: np.asarray(a) for name, a in inputs.items()}
    ids = x["ids"].reshape(ROWS, TILES, F).transpose(0, 2, 1).reshape(P, TILES)
    w = x["L0_rec_Ws"].reshape(LAYERS, F, EC, P).transpose(3, 0, 2, 1)
    w_cols = np.zeros((P, LAYERS, EC, 2, 2 * F), w.dtype)
    w_cols[:, :, :, 0, :F] = w
    w_cols[:, :, :, 1, F:] = w
    const = shape_constants()
    arrays = {
        "tables": np.concatenate([x[f"tbl_{i}"] for i in range(F)], axis=0),
        "ids_t": ids, "id_limits": const["id_limits"],
        "w_cols": w_cols, "biases": np.tile(x["L0_rec_bs"].T, (ROWS, 1)),
        "ident": const["ident"], "block_ones": const["block_ones"], "own_field": const["own_field"],
        "ones": const["ones"], "unpack_sel": const["unpack_sel"], "dense_t": x["dense_ctx"].T,
        "w_top1": x["W_top1"], "b_top1": x["b_top1"].reshape(1, HID1), "b_cols1": x["b_top1"].reshape(H1, P).T,
        "w_top2": x["W_top2"].reshape(H1, P, HID2).transpose(1, 0, 2), "b_top2": x["b_top2"].reshape(1, HID2), "b_cols2": x["b_top2"].reshape(H2, P).T,
        "w_top3": x["W_top3"].reshape(H2, P).T,
    }
    arrays = {name: np.ascontiguousarray(a) for name, a in arrays.items()}
    nc = bacc.Bacc("TRN2", target_bir_lowering=False, num_devices=1)
    args = [nc.dram_tensor(name, a.shape, mybir.dt.from_np(a.dtype), kind="ExternalInput").ap() for name, a in arrays.items()]
    y = nc.dram_tensor("y", (1, BATCH), FP32, kind="ExternalOutput").ap()
    build(nc, *args, y)
    r = run_bass_kernel_spmd(nc, [arrays], core_ids=[0])
    return r.results[0]["y"].reshape(BATCH, 1)
```
